# Optimizing a Trainium2 kernel written in Bass

```python
import numpy as np
import jax
import jax.numpy as jnp

def _softmax(x, axis=-1):
    return jax.nn.softmax(x, axis=axis)
def _gelu(x):
    return jax.nn.gelu(x, approximate=True)
def _silu(x):
    return jax.nn.silu(x)
def _sigmoid(x):
    return jax.nn.sigmoid(x)
def _layernorm(x, axis=-1, eps=1e-5):
    m = jnp.mean(x, axis=axis, keepdims=True)
    v = jnp.var(x, axis=axis, keepdims=True)
    return (x - m) / jnp.sqrt(v + eps)
def _scatter_add(tgt, idx, src, axis=0):
    return tgt.at[idx].add(src)
def _segment_sum(src, seg, n):
    return jax.ops.segment_sum(src, seg, n)

kernel_name = 'mk_conv_preact_d2_conv_nchw96_a1db49'

def setup_inputs(seed: int = 0):
    np.random.seed(seed)
    _w = jnp.asarray
    def _rec_inputs():
        import jax
        import jax.numpy as jnp
        _gk = jax.random.key(seed)
        x = -0.0001476 + 0.9999 * jax.random.normal(jax.random.fold_in(_gk, 1), (32, 96, 112, 112), jnp.float32)
        return x
    x = _rec_inputs()
    def _L0_conv_setup():
        import jax, jax.numpy as jnp
        import numpy as np
        B, C, H, W = (32, 96, 112, 112)
        GROUPS = 6
        SQUEEZE = 24
        EXP = 4
        INIT_A = (0.0, 0.0)
        INIT_B = (0.0, 0.0)

        def _shift_index(channels: int, groups: int) -> jnp.ndarray:
            cpg = channels // groups
            idx = jnp.arange(channels).reshape(groups, cpg)
            idx = jnp.concatenate([idx[1:], idx[:1]], axis=0)
            idx = jnp.concatenate([idx[:, 1:], idx[:, :1]], axis=1)
            return idx.reshape(channels)

        def _hardsigmoid(v):
            return jnp.clip(v / 6.0 + 0.5, 0.0, 1.0)
        key = jax.random.key(seed)
        k1, k2, k3, k4, k5 = jax.random.split(key, 5)
        x = jax.random.normal(k1, (B, C, H, W), dtype=jnp.float32)
        W1 = jax.random.normal(k2, (SQUEEZE, C), dtype=jnp.float32) * 0.1
        b1 = jax.random.normal(k3, (SQUEEZE,), dtype=jnp.float32) * 0.1
        W2 = jax.random.normal(k4, (C * EXP, SQUEEZE), dtype=jnp.float32) * 0.1
        b2 = jax.random.normal(k5, (C * EXP,), dtype=jnp.float32) * 0.1
        return {'x': x, 'W1': W1, 'b1': b1, 'W2': W2, 'b2': b2}
    _L0_conv_all = _L0_conv_setup()
    _L0_conv_in = {k: v for k, v in _L0_conv_all.items() if k in ('W1', 'b1', 'W2', 'b2', )}
    del _L0_conv_all

    def _L1_conv_setup():
        import jax, jax.numpy as jnp
        import numpy as np
        K_CONST = 2.0
        KERNEL = 5
        ALPHA = 0.0001
        BETA = 0.75
        key = jax.random.key(seed)
        x = jax.random.normal(key, (16, 96, 224, 224), dtype=jnp.float32)
        return {'x': x}
    _L1_conv_all = _L1_conv_setup()
    _L1_conv_in = {k: v for k, v in _L1_conv_all.items() if k in ()}
    del _L1_conv_all

    return {
        "x": x,
        "L0_conv_W1": _L0_conv_in["W1"],
        "L0_conv_b1": _L0_conv_in["b1"],
        "L0_conv_W2": _L0_conv_in["W2"],
        "L0_conv_b2": _L0_conv_in["b2"],
    }

def reference(x, L0_conv_W1, L0_conv_b1, L0_conv_W2, L0_conv_b2):
    import jax
    import jax.numpy as jnp
    def _L0_conv_ref(x, W1, b1, W2, b2):
        import jax, jax.numpy as jnp
        import numpy as np
        B, C, H, W = (32, 96, 112, 112)
        GROUPS = 6
        SQUEEZE = 24
        EXP = 4
        INIT_A = (0.0, 0.0)
        INIT_B = (0.0, 0.0)

        def _shift_index(channels: int, groups: int) -> jnp.ndarray:
            cpg = channels // groups
            idx = jnp.arange(channels).reshape(groups, cpg)
            idx = jnp.concatenate([idx[1:], idx[:1]], axis=0)
            idx = jnp.concatenate([idx[:, 1:], idx[:, :1]], axis=1)
            return idx.reshape(channels)

        def _hardsigmoid(v):
            return jnp.clip(v / 6.0 + 0.5, 0.0, 1.0)
        index = _shift_index(C, GROUPS)
        y = jnp.mean(x, axis=(2, 3))
        h = jax.nn.relu(y @ W1.T + b1)
        y = _hardsigmoid(h @ W2.T + b2)
        y = (y - 0.5) * 4.0
        a1, bb1, a2, bb2 = jnp.split(y, 4, axis=1)
        a1 = (a1 + INIT_A[0])[:, :, None, None]
        a2 = (a2 + INIT_B[1])[:, :, None, None]
        bb1 = (bb1 + INIT_B[0])[:, :, None, None]
        bb2 = (bb2 + INIT_B[1])[:, :, None, None]
        x2 = x[:, index, :, :]
        z1 = x * a1 + x2 * bb1
        z2 = x * a2 + x2 * bb2
        return jnp.maximum(z1, z2)

    def _L1_conv_ref(x):
        import jax, jax.numpy as jnp
        import numpy as np
        K_CONST = 2.0
        KERNEL = 5
        ALPHA = 0.0001
        BETA = 0.75
        s = jnp.sum(x * x, axis=1, keepdims=True)
        w = jnp.ones((1, 1, KERNEL, KERNEL), dtype=x.dtype)
        y = jax.lax.conv_general_dilated(s, w, window_strides=(1, 1), padding='SAME', dimension_numbers=('NCHW', 'OIHW', 'NCHW'))
        return x / (K_CONST + ALPHA * y) ** BETA

    def _gn(v, G=32, eps=1e-5):
        B_, C_, H_, W_ = v.shape
        g = v.reshape(B_, G, C_ // G, H_, W_)
        m = jnp.mean(g, axis=(2, 3, 4), keepdims=True)
        s = jnp.var(g, axis=(2, 3, 4), keepdims=True)
        return ((g - m) / jnp.sqrt(s + eps)).reshape(v.shape)

    def _ln_c(v, eps=1e-6):
        m = jnp.mean(v, axis=1, keepdims=True)
        s = jnp.var(v, axis=1, keepdims=True)
        return (v - m) / jnp.sqrt(s + eps)

    def _ln_t(v, eps=1e-5):
        m = jnp.mean(v, axis=-1, keepdims=True)
        s = jnp.var(v, axis=-1, keepdims=True)
        return (v - m) / jnp.sqrt(s + eps)

    def _to_tokens(v):
        B_, C_, H_, W_ = v.shape
        return v.reshape(B_, C_, H_ * W_).transpose(0, 2, 1)
    def _from_tokens(t, like):
        B_, C_, H_, W_ = like.shape
        return t.transpose(0, 2, 1).reshape(B_, C_, H_, W_)

    x = x + _L0_conv_ref(_gn(x), L0_conv_W1, L0_conv_b1, L0_conv_W2, L0_conv_b2)
    x = x + _L1_conv_ref(_gn(x))
    return x


_drawn_inputs = setup_inputs


def setup_inputs(seed=0):
    import zlib

    import numpy as np

    out = dict(_drawn_inputs(seed))
    spreads = {}
    factors = {'L0_conv_W1': 28.439}
    for name, (base, spread) in spreads.items():
        noise = np.random.default_rng([zlib.crc32(name.encode()), seed]).standard_normal(out[name].shape)
        drawn = base * np.exp(spread * noise) if base else spread * noise
        out[name] = jnp.asarray(drawn.astype(out[name].dtype))
    for name, factor in factors.items():
        out[name] = (out[name] * factor).astype(out[name].dtype)
    return out
```

```python
from contextlib import ExitStack

import numpy as np
import concourse.bass as bass
from concourse import mybir

B, C, H, W = 32, 96, 112, 112
HW = H * W
GROUPS = 32
J = C // GROUPS
Q = 4
QROWS = H // Q
QN = HW // Q
ROWS = 4
BW = ROWS * W
NB = QN // BW
P = 128
SQ = 24
PARTS = 4
ONES = C
EPS = 1e-5
K_CONST, ALPHA = 2.0, 1e-4
LEAD = 2
LAG = 1

COEF = ["aggr", "gmean", "dneg", "nmean", "negk", "spread", "gvar", "veps", "rs", "y", "hid_ps", "hid",
        "mlp_ps", "mlp", "scaled", "coef", "p0", "p1", "i0", "i1", "whole", "crow_ps", "crow"]
NORM = ["gsum", "reduced", "dev", "ndev2", "veps", "rs", "nbias"]
BOX = ["evac0", "evac1", "vert_ps", "vert", "full_ps", "t", "root", "t_root", "root2", "d0",
       "w", "w2", "a", "e", "g", "d", "hi", "lo"]


def build(nc, x, w1t, b1, w2t, b2, eye, shift, g96, g96k, g128, quarter, vband, band, onehot, out):
    f32, f16, f8 = mybir.dt.float32, mybir.dt.float16, mybir.dt.float8e4
    ALU, ACT = mybir.AluOpType, mybir.ActivationFunctionType
    AX = mybir.AxisListType

    x_v = x.rearrange("n c h w -> n c (h w)").rearrange("n c (q b m) -> n b c q m", q=Q, b=NB)
    out_v = out.rearrange("n c h w -> n c (h w)").rearrange("n (r j) (q b m) -> n b q r j m", j=J, q=Q, b=NB)

    ctx = ExitStack()
    with ctx:
        def sb(name, shape, dt=f32):
            return ctx.enter_context(nc.sbuf_tensor(name, shape, dt))

        def ps(name, shape):
            return ctx.enter_context(nc.psum_tensor(name, shape, f32))

        def sem(name):
            return ctx.enter_context(nc.semaphore(name))

        xin = [sb(f"xin{p}", [P, NB, Q, BW]) for p in range(2)]
        x1 = [sb(f"x1_{p}", [P, NB, J, BW]) for p in range(2)]
        squares = [sb(f"squares{p}", [P, J, BW]) for p in range(2)]
        f1_sb = sb("f1_sb", [P, J, BW])
        s_sb = sb("s_sb", [P, NB, W])
        eye_sb = sb("eye_sb", [C, C], f16)
        shift_sb = sb("shift_sb", [C, C], f16)
        g96_sb = sb("g96_sb", [C, C])
        g96k_sb = sb("g96k_sb", [C, P])
        g128_sb = sb("g128_sb", [P, P])
        quarter_sb = sb("quarter_sb", [P, 32])
        vband_sb = sb("vband_sb", [P, NB, H])
        band_sb = sb("band_sb", [W, W])
        onehot_sb = sb("onehot_sb", [H, QROWS, Q, 32], f8)
        w1t_sb = sb("w1t_sb", [C, SQ])
        w2t_sb = sb("w2t_sb", [SQ, PARTS, C])
        b1_sb = sb("b1_sb", [SQ, 1])
        b2_sb = sb("b2_sb", [C, PARTS])
        minus_half = sb("minus_half", [P, 1])
        onehot_f = s_sb[0:H, 0, :].rearrange("p (o q) -> p o q", q=Q)
        bn = sb("bn", [C, NB * Q, 6])
        mv = sb("mv", [C, 2])
        dneg, nmean, spread, veps, rs, y = (sb(n, [C, 1]) for n in ("dneg", "nmean", "spread", "veps", "rs", "y"))
        negk = [sb(f"negk{p}", [P, 1]) for p in range(2)]
        hid = sb("hid", [SQ, 1])
        mlp, scaled, coef = (sb(n, [C, PARTS]) for n in ("mlp", "scaled", "coef"))
        wprime = sb("wprime", [C, 2, C])
        wmix = [sb(f"wmix{p}", [P, 2, J, GROUPS]) for p in range(2)]
        sums = [sb(f"sums{p}", [P, 2, NB]) for p in range(2)]
        me = [sb(f"me{p}", [P, 2]) for p in range(2)]
        dev, ndev2, veps1 = (sb(n, [P, 1]) for n in ("dev", "ndev2", "veps1"))
        rs1 = [sb(f"rs1_{p}", [P, 1]) for p in range(2)]
        nbias = [sb(f"nbias{p}", [P, 1]) for p in range(2)]
        box = {n: sb(f"box_{n}", [H, W]) for n in ("t", "root", "w2", "d0")}
        box |= {"vert": box["t"], "t_root": box["root"], "root2": box["root"], "w": box["root"],
                "a": box["root"], "e": box["w2"], "g": box["root"], "d": box["w2"]}
        d_hi, d_lo = sb("d_hi", [H, W], f16), sb("d_lo", [H, W], f16)

        f1 = ps("f1", [P, J, 512])
        f2 = ps("f2", [P, J, 512])
        shared = ps("shared", [P, 512])
        d_wide = ps("d_wide", [P, 512])

        pool_passed, dve_passed, pe_passed = sem("pool_passed"), sem("dve_passed"), sem("pe_passed")
        consts_in = sem("consts_in")
        rows_set = sem("rows_set")
        ones_set = sem("ones_set")
        onehot_set = sem("onehot_set")
        loaded = [[sem(f"loaded{p}_{b}") for b in range(NB)] for p in range(2)]
        stored = [[sem(f"stored{p}_{b}") for b in range(NB)] for p in range(2)]
        bn_done = sem("bn_done")
        coef_link = sem("coef_link")
        norm_link = sem("norm_link")
        box_link = sem("box_link")
        f1_ready = sem("f1_ready")
        f1_evacuated = sem("f1_evacuated")
        f2_ready = sem("f2_ready")
        x1_ready = sem("x1_ready")
        sumsq_ready = sem("sumsq_ready")
        squares_ready = sem("squares_ready")
        chansum_ready = sem("chansum_ready")
        d_ready = sem("d_ready")
        e_ready = sem("e_ready")
        scaled_ready = sem("scaled_ready")
        result_ready = sem("result_ready")

        CONSTS = [(eye_sb, eye), (shift_sb, shift), (g96_sb, g96), (g96k_sb, g96k), (g128_sb, g128),
                  (quarter_sb, quarter), (vband_sb, vband), (band_sb, band), (onehot_f, onehot),
                  (w1t_sb, w1t), (w2t_sb, w2t), (b1_sb, b1), (b2_sb, b2)]

        def count(img, per_image, more):
            k, p = img
            return k * (2 * per_image) + (per_image * p + more)

        def wait(eng, semaphore, img, per_image, more):
            v = count(img, per_image, more)
            if not isinstance(v, int) or v > 0:
                eng.wait_ge(semaphore, v)

        def wait_apart(eng, semaphore, img, per_image, more, passed):
            v = count(img, per_image, more)
            if isinstance(v, int):
                if v > 0:
                    eng.wait_ge(semaphore, v)
            else:
                eng.wait_ge(semaphore, v)
                eng.sem_inc(passed, 1)

        def after(eng, chain, semaphore, img, link):
            wait(eng, semaphore, img, len(chain), chain.index(link) + 1)

        def begins(eng, chain, semaphore, img):
            wait(eng, semaphore, img, len(chain), 0)

        def plus(img, n):
            k, p = img
            return (k + (p + n) // 2, (p + n) % 2)

        def exists(img):
            k, p = img
            return not isinstance(k, int) or 0 <= 2 * k + p < B

        FIRST, LAST = -2, B + 1
        LOOP = (1, B // 2 - 1)

        def iterations(eng, body):
            for n in range(FIRST, 2 * LOOP[0]):
                body((n // 2, n % 2))
            with eng.Fori(*LOOP) as k:
                body((k, 0))
                body((k, 1))
            for n in range(2 * LOOP[1], LAST + 1):
                body((n // 2, n % 2))

        def ahead(img, b):
            return (plus(img, 1), b + LEAD) if b + LEAD < NB else (plus(img, 2), b + LEAD - NB)

        def behind(img, b):
            return (plus(img, -2), b + LAG) if b + LAG < NB else (plus(img, -1), b + LAG - NB)

        def before(img, b):
            return (img, b - 1) if b else (plus(img, -1), NB - 1)

        SQUARES_AT = {0: [0], 1: [1, 2], 2: [3, 4], 3: [5, 6]}
        SUM_BETWEEN = {1: 0, 2: 2, 3: 4, 4: 6}
        SUM_AFTER = {1: 1, 2: 3, 3: 5}

        block = ctx.enter_context(nc.Block())

        @block.sync
        def _(sp):
            def load(img, b):
                wait(sp, f2_ready, plus(img, -2), NB, b + 1)
                k, p = img
                sp.dma_start(xin[p][0:C, b], x_v[2 * k + p, b]).then_inc(loaded[p][b], 16)

            def store(img, b):
                wait(sp, result_ready, img, NB, b + 1)
                k, p = img
                for q in range(Q):
                    sp.dma_start(out_v[2 * k + p, b, q], x1[p][32 * q:32 * q + 32, b]).then_inc(stored[p][b], 16)

            for b in range(2):
                load((0, 0), b)
            for dst, src in CONSTS:
                sp.dma_start(dst[tuple(slice(None) for _ in dst.shape)], src).then_inc(consts_in, 16)
            for b in range(2, NB):
                load((0, 0), b)
            for b in range(NB):
                load((0, 1), b)

            def body(img):
                for b in range(NB):
                    old, ob = behind(img, b)
                    if exists(old):
                        store(old, ob)
                    nxt = plus(img, 2)
                    if exists(img) and exists(nxt):
                        load(nxt, b)

            iterations(sp, body)
            for p in range(2):
                for b in range(NB):
                    sp.wait_ge(stored[p][b], 16 * Q * (B // 2))

        @block.gpsimd
        def _(pool):
            for n in range(2):
                if n:
                    pool.wait_ge(rows_set, n)
                nc.gpsimd.memset(wmix[n][C:P], 0.0).then_inc(rows_set, 1)
            pool.wait_ge(rows_set, 2)
            nc.gpsimd.memset(minus_half[:], -0.5).then_inc(rows_set, 1)
            pool.wait_ge(rows_set, 3)
            for n in range(2):
                if n:
                    pool.wait_ge(ones_set, n)
                nc.gpsimd.memset(xin[n][C:P], 1.0).then_inc(ones_set, 1)
            pool.wait_ge(ones_set, 2)

            def body(img):
                for b in range(NB):
                    old, ob = behind(img, b)
                    prev, nxt = plus(img, -1), plus(img, 1)
                    if exists(old):
                        wait(pool, result_ready, old, NB, ob)
                    if b == 0 and exists(prev):
                        p = prev[1]
                        after(pool, NORM, norm_link, prev, "veps")
                        nc.gpsimd.tensor_tensor(rs1[p][:], veps1[:], minus_half[:], ALU.pow).then_inc(norm_link, 1)
                        after(pool, NORM, norm_link, prev, "rs")
                    if b == 5 and exists(nxt):
                        after(pool, COEF, coef_link, nxt, "veps")
                        nc.gpsimd.tensor_tensor(rs[:], veps[:], minus_half[0:C], ALU.pow).then_inc(coef_link, 1)
                        after(pool, COEF, coef_link, nxt, "rs")
                    if exists(old):
                        p = old[1]
                        wait_apart(pool, scaled_ready, old, NB, ob + 1, pool_passed)
                        nc.gpsimd.tensor_scalar(x1[p][:, ob], x1[p][:, ob], 1.0, me[p][:, 0:1],
                                                ALU.mult, ALU.add).then_inc(result_ready, 1)

            iterations(pool, body)

        @block.scalar
        def _(act):
            def evacuate(img, b):
                wait(act, sumsq_ready, img, NB, b)
                wait(act, f1_ready, img, NB, b + 1)
                nc.scalar.activation(f1_sb[:], f1[:, :, 0:BW], ACT.Identity).then_inc(f1_evacuated, 1)

            def sum_squares(img, b):
                p = img[1]
                wait(act, x1_ready, img, NB, b + 1)
                if b == 0:
                    after(act, COEF, coef_link, img, "negk")
                nc.scalar.activation(f1_sb[:], x1[p][:, b], ACT.Square, bias=negk[p][:, 0:1],
                                     accum_out=sums[p][:, 1, b:b + 1]).then_inc(sumsq_ready, 1)

            def normalised_squares(img, b):
                p = img[1]
                if b == 0:
                    after(act, NORM, norm_link, img, "nbias")
                wait(act, chansum_ready, img, NB, b - 1)
                buf = squares[(NB * p + b) % 2]
                nc.scalar.activation(buf[:], x1[p][:, b], ACT.Square, bias=nbias[p][:, 0:1],
                                     scale=rs1[p][:, 0:1]).then_inc(squares_ready, 1)

            def factor(img, b):
                p = img[1]
                wait(act, d_ready, img, NB, b + 1)
                nc.scalar.activation(d_wide[:, 0:BW], d_wide[:, 0:BW], ACT.Identity, bias=1.0,
                                     scale=rs1[p][:, 0:1]).then_inc(e_ready, 1)

            def root(img, src, dst):
                after(act, BOX, box_link, img, src)
                nc.scalar.activation(box[dst][:], box[src][:], ACT.Sqrt).then_inc(box_link, 1)

            def body(img):
                prev = plus(img, -1)
                for b in range(NB):
                    old, ob = behind(img, b)
                    done, db = before(img, b)
                    if exists(old) and ob > 0:
                        factor(old, ob)
                    if exists(done):
                        sum_squares(done, db)
                    if b == 5 and exists(prev):
                        root(prev, "t", "root")
                    if exists(img):
                        evacuate(img, b)
                    if b == 5 and exists(prev):
                        root(prev, "t_root", "root2")
                    if exists(old) and ob == 0:
                        factor(old, ob)
                    if exists(prev):
                        for sb_ in SQUARES_AT.get(b, []):
                            normalised_squares(prev, sb_)

            iterations(act, body)

        @block.vector
        def _(dve):
            V = nc.vector

            def statistics(img, b):
                k, p = img
                dve.wait_ge(loaded[p][b], k * 16 + 16)
                if b == 0:
                    after(dve, COEF, coef_link, plus(img, -1), "aggr")
                for q in range(Q):
                    V.bn_stats(bn[:, b * Q + q], xin[p][0:C, b, q]).then_inc(bn_done, 1)

            def link(chain, semaphore, img, name, ins_of):
                wait(dve, semaphore, img, len(chain), chain.index(name))
                ins_of().then_inc(semaphore, 1)

            def coef_begin(img):
                begins(dve, COEF, coef_link, img)
                wait_apart(dve, bn_done, img, NB * Q, NB * Q, dve_passed)
                V.bn_aggr(mv[:], bn[:]).then_inc(coef_link, 1)

            def coef_centre(img):
                p = img[1]

                def c(name, ins_of):
                    link(COEF, coef_link, img, name, ins_of)

                c("dneg", lambda: V.tensor_scalar(dneg[:], shared[0:C, 0:1], mv[:, 0:1], None, ALU.subtract))
                c("nmean", lambda: V.tensor_scalar(nmean[:], shared[0:C, 0:1], -1.0, None, ALU.mult))
                c("negk", lambda: V.tensor_scalar(negk[p][:], shared[:, 1:2], -1.0, None, ALU.mult))
                c("spread", lambda: V.scalar_tensor_tensor(out=spread[:], in0=dneg[:], scalar=dneg[:, 0:1],
                                                           in1=mv[:, 1:2], op0=ALU.mult, op1=ALU.add))

            def coef_y(img):
                def c(name, ins_of):
                    link(COEF, coef_link, img, name, ins_of)

                c("veps", lambda: V.tensor_scalar(veps[:], shared[0:C, 2:3], EPS, None, ALU.add))

                c("y", lambda: V.tensor_scalar(y[:], dneg[:], rs[:, 0:1], -1.0, ALU.mult, ALU.mult))

            def coef_hid(img):
                def c(name, ins_of):
                    link(COEF, coef_link, img, name, ins_of)

                c("hid", lambda: V.tensor_scalar(hid[:], shared[0:SQ, 3:4], b1_sb[:, 0:1], 0.0, ALU.add, ALU.max))

            def coef_end(img):
                p = img[1]

                def c(name, ins_of):
                    link(COEF, coef_link, img, name, ins_of)

                c("mlp", lambda: V.tensor_tensor(mlp[:], shared[0:C, 4:4 + PARTS], b2_sb[:], ALU.add))
                c("scaled", lambda: V.tensor_scalar(scaled[:], mlp[:], 2.0 / 3.0, -2.0, ALU.mult, ALU.max))
                c("coef", lambda: V.tensor_scalar(coef[:], scaled[:], 2.0, rs[:, 0:1], ALU.min, ALU.mult))

                for i in range(2):
                    c(f"p{i}", lambda: V.tensor_scalar(wprime[:, i], shift_sb[:], coef[:, 2 * i + 1:2 * i + 2],
                                                       None, ALU.mult))
                for i in range(2):
                    c(f"i{i}", lambda: V.scalar_tensor_tensor(
                        out=wprime[:, i], in0=eye_sb[:], scalar=coef[:, 2 * i:2 * i + 1], in1=wprime[:, i],
                        op0=ALU.mult, op1=ALU.add))
                wait(dve, f2_ready, plus(img, -1), NB, 0)
                c("whole", lambda: V.tensor_tensor(
                    wmix[p][0:C].rearrange("k i j r -> k i (j r)"), wprime[:],
                    eye_sb[:, None, :].to_broadcast([C, 2, C]), ALU.add))

            def coef_row(img):
                p = img[1]

                def c(name, ins_of):
                    link(COEF, coef_link, img, name, ins_of)

                c("crow", lambda: V.tensor_copy(wmix[p][ONES:ONES + 1].rearrange("k i j r -> k (i j r)"),
                                                shared[ONES:ONES + 1, 64:64 + 2 * C]))

            def maximum(img, b):
                p = img[1]
                if not isinstance(img[0], int) or img[0] > 0:
                    dve.wait_ge(stored[p][b], img[0] * (16 * Q))
                wait(dve, f1_evacuated, img, NB, b + 1)
                wait(dve, f2_ready, img, NB, b + 1)
                V.scalar_tensor_tensor(out=x1[p][:, b], in0=f2[:, :, 0:BW], scalar=0.0, in1=f1_sb[:],
                                       op0=ALU.add, op1=ALU.max,
                                       accum_out=sums[p][:, 0, b:b + 1]).then_inc(x1_ready, 1)

            def norm(img):
                p = img[1]

                def c(name, ins_of):
                    link(NORM, norm_link, img, name, ins_of)

                c("reduced", lambda: V.tensor_reduce(
                    me[p][:], shared[:, 256:256 + 2 * NB].rearrange("p (s b) -> p s b", s=2), AX.X, ALU.add))
                c("dev", lambda: V.tensor_scalar(dev[:], me[p][:, 0:1], negk[p][:, 0:1], None, ALU.add))
                c("ndev2", lambda: V.tensor_scalar(ndev2[:], dev[:], dev[:, 0:1], -1.0, ALU.mult, ALU.mult))
                c("veps", lambda: V.scalar_tensor_tensor(out=veps1[:], in0=me[p][:, 1:2], scalar=EPS, in1=ndev2[:],
                                                         op0=ALU.add, op1=ALU.add))
                c("nbias", lambda: V.tensor_scalar(nbias[p][:], me[p][:, 0:1], rs1[p][:, 0:1], -1.0,
                                                   ALU.mult, ALU.mult))

            def box_step(img, name, ins_of):
                link(BOX, box_link, img, name, ins_of)

            def evacuate_sums(img, half):
                b0, b1_ = (0, 4) if half == 0 else (4, NB)
                wait(dve, chansum_ready, img, NB, b1_)
                box_step(img, f"evac{half}", lambda: V.tensor_copy(
                    s_sb[:, b0:b1_], shared[:, 0:(b1_ - b0) * W].rearrange("p (b w) -> p b w", w=W)))

            def box_vert(img):
                box_step(img, "vert", lambda: V.tensor_copy(box["vert"][:], shared[0:W, 0:H]))

            def tt(img, o, a, b):
                box_step(img, o, lambda: V.tensor_tensor(box[o][:], box[a][:], box[b][:], ALU.mult))

            def box_t(img):
                box_step(img, "t", lambda: V.tensor_scalar(box["t"][:], shared[0:H, 128:128 + W], ALPHA, K_CONST,
                                                           ALU.mult, ALU.add))

            def box_power(img):
                box_step(img, "d0", lambda: V.reciprocal(box["d0"][:], box["root2"][:]))
                tt(img, "w", "t", "d0")
                tt(img, "w2", "w", "w")
                tt(img, "a", "w", "d0")
                tt(img, "e", "w2", "a")
                box_step(img, "g", lambda: V.tensor_scalar(box["g"][:], box["e"][:], -0.25, 1.25, ALU.mult, ALU.add))
                tt(img, "d", "d0", "g")
                wait(dve, d_ready, img, NB, 0)
                box_step(img, "hi", lambda: V.tensor_copy(d_hi[:], box["d"][:]))
                box_step(img, "lo", lambda: V.tensor_tensor(d_lo[:], box["d"][:], d_hi[:], ALU.subtract))

            def scale(img, b):
                p = img[1]
                wait(dve, e_ready, img, NB, b + 1)
                V.scalar_tensor_tensor(out=x1[p][:, b], in0=x1[p][:, b], scalar=me[p][:, 0:1],
                                       in1=d_wide[:, None, 0:BW].to_broadcast([P, J, BW]),
                                       op0=ALU.subtract, op1=ALU.mult).then_inc(scaled_ready, 1)

            dve.wait_ge(consts_in, 16 * len(CONSTS))
            V.tensor_copy(onehot_sb[:], onehot_f[:, :, :, None].to_broadcast([H, QROWS, Q, 32]),
                          saturate=False).then_inc(onehot_set, 1)
            dve.wait_ge(rows_set, 3)

            def body(img):
                prev, nxt = plus(img, -1), plus(img, 1)
                for b in range(NB):
                    old, ob = behind(img, b)
                    done, db = before(img, b)
                    new, nb = ahead(img, b)
                    if exists(done):
                        maximum(done, db)
                    if b == 3 and exists(prev):
                        evacuate_sums(prev, 0)
                    if b == 5 and exists(prev):
                        box_t(prev)
                    if b == 6 and exists(nxt):
                        coef_end(nxt)
                    if exists(old):
                        scale(old, ob)
                    if b == 0 and exists(prev):
                        norm(prev)
                    if b == 4 and exists(prev):
                        evacuate_sums(prev, 1)
                    if b == 5 and exists(nxt):
                        coef_centre(nxt)
                    if b == 5 and exists(prev):
                        tt(prev, "t_root", "t", "root")
                    if b == 5 and exists(nxt):
                        coef_y(nxt)
                    if b == 6 and exists(nxt):
                        coef_row(nxt)
                    if exists(new):
                        statistics(new, nb)
                    if b == 5 and exists(nxt):
                        coef_hid(nxt)
                    if b == 5 and exists(prev):
                        box_power(prev)
                    if b == 4 and exists(prev):
                        box_vert(prev)
                    if b == 4 and exists(nxt):
                        coef_begin(nxt)

            iterations(dve, body)

        @block.tensor
        def _(pe):
            T = nc.tensor

            def mix(img, b, i):
                p = img[1]
                if b == 0 and i == 0:
                    after(pe, COEF, coef_link, img, "crow")
                if i == 0:
                    wait(pe, f1_evacuated, img, NB, b)
                else:
                    wait(pe, x1_ready, img, NB, b)
                dst = (f1, f2)[i]
                for j in range(J):
                    for q in range(Q):
                        last = T.matmul(dst[32 * q:32 * q + 32, j, 0:BW], wmix[p][:, i, j, :], xin[p][:, b, q, :],
                                        start=True, stop=True)
                last.then_inc((f1_ready, f2_ready)[i], 1)

            def coef_groups(img):
                after(pe, BOX, box_link, plus(img, -2), "t")
                after(pe, COEF, coef_link, img, "aggr")
                T.matmul(shared[0:C, 0:1], g96_sb[:], mv[:, 0:1], start=True, stop=True)
                T.matmul(shared[:, 1:2], g96k_sb[:], mv[:, 0:1], start=True, stop=True).then_inc(coef_link, 1)
                after(pe, COEF, coef_link, img, "spread")
                T.matmul(shared[0:C, 2:3], g96_sb[:], spread[:], start=True, stop=True).then_inc(coef_link, 1)

            def coef_y(img):
                after(pe, COEF, coef_link, img, "y")
                T.matmul(shared[0:SQ, 3:4], w1t_sb[:], y[:], start=True, stop=True).then_inc(coef_link, 1)

            def coef_mlp(img):
                after(pe, COEF, coef_link, img, "hid")
                for s in range(PARTS):
                    last = T.matmul(shared[0:C, 4 + s:5 + s], w2t_sb[:, s, :], hid[:], start=True, stop=True)
                last.then_inc(coef_link, 1)

            def coef_row(img):
                after(pe, COEF, coef_link, img, "whole")
                T.matmul(shared[ONES:ONES + 1, 64:64 + 2 * C], nmean[:], wprime[:].rearrange("k i c -> k (i c)"),
                         start=True, stop=True).then_inc(coef_link, 1)

            def group_sums(img):
                wait(pe, x1_ready, img, NB, NB)
                wait(pe, sumsq_ready, img, NB, NB)
                begins(pe, NORM, norm_link, img)
                T.matmul(shared[:, 256:256 + 2 * NB], g128_sb[:], sums[img[1]][:].rearrange("p s b -> p (s b)"),
                         start=True, stop=True).then_inc(norm_link, 1)

            def channel_sum(img, b):
                wait(pe, squares_ready, img, NB, b + 1)
                if b == 4:
                    after(pe, BOX, box_link, img, "evac0")
                buf = squares[(NB * img[1] + b) % 2]
                at = (b % 4) * W
                for j in range(J):
                    for t in range(ROWS):
                        last = T.matmul(shared[32 * t:32 * t + 32, at:at + W], quarter_sb[:], buf[:, j, t * W:t * W + W],
                                        start=(j == 0), stop=(j == J - 1))
                last.then_inc(chansum_ready, 1)

            def box_vert(img):
                after(pe, BOX, box_link, img, "evac1")
                for b in range(NB):
                    last = T.matmul(shared[0:W, 0:H], s_sb[:, b, :], vband_sb[:, b, :], start=(b == 0), stop=(b == NB - 1))
                last.then_inc(box_link, 1)

            def box_full(img):
                after(pe, BOX, box_link, img, "vert")
                T.matmul(shared[0:H, 128:128 + W], box["vert"][:], band_sb[:], start=True, stop=True).then_inc(box_link, 1)

            def spread_d(img, b):
                if b == 0:
                    after(pe, BOX, box_link, img, "lo")
                wait_apart(pe, scaled_ready, img, NB, b, pe_passed)
                for t in range(ROWS):
                    rows = onehot_sb[:, ROWS * b + t].rearrange("h q r -> h (q r)")
                    for half in (d_hi, d_lo):
                        last = T.matmul(d_wide[:, t * W:t * W + W], rows, half[:], start=(half is d_hi),
                                        stop=(half is d_lo))
                last.then_inc(d_ready, 1)

            pe.wait_ge(consts_in, 16 * len(CONSTS))
            pe.wait_ge(onehot_set, 1)
            pe.wait_ge(ones_set, 2)

            def body(img):
                prev, nxt = plus(img, -1), plus(img, 1)
                for b in range(NB):
                    old, ob = behind(img, b)
                    if exists(old) and ob > 0:
                        spread_d(old, ob)
                    if b == 6 and exists(nxt):
                        coef_mlp(nxt)
                    if exists(img):
                        mix(img, b, 0)
                    if b == 0 and exists(prev):
                        group_sums(prev)
                    if b in SUM_BETWEEN and exists(prev):
                        channel_sum(prev, SUM_BETWEEN[b])
                    if b == 4 and exists(prev):
                        box_vert(prev)
                    if b == 5 and exists(nxt):
                        coef_groups(nxt)
                    if exists(old) and ob == 0:
                        spread_d(old, ob)
                    if b == 6 and exists(nxt):
                        coef_row(nxt)
                    if exists(img):
                        mix(img, b, 1)
                    if b in SUM_AFTER and exists(prev):
                        channel_sum(prev, SUM_AFTER[b])
                    if b == 4 and exists(prev):
                        box_full(prev)
                    if b == 5 and exists(nxt):
                        coef_y(nxt)

            iterations(pe, body)


def constants():
    cg = C // 6
    idx = np.arange(C).reshape(6, cg)
    idx = np.concatenate([idx[1:], idx[:1]], axis=0)
    idx = np.concatenate([idx[:, 1:], idx[:, :1]], axis=1).reshape(C)
    chan = np.array([J * r + j for j in range(J) for r in range(GROUPS)])
    f = np.float32
    k = np.arange(C)[:, None]
    eye = (k == chan[None, :]).astype(np.float16)
    shift = (k == idx[chan][None, :]).astype(np.float16)
    g96 = (k // J == k.T // J).astype(f) / f(J)
    part = np.arange(P)
    g96k = (k // J == part[None, :] % GROUPS).astype(f) / f(J)
    g128 = (part[:, None] % GROUPS == part[None, :] % GROUPS).astype(f) / f(J * HW)
    quarter = (part[:, None] // GROUPS == np.arange(32)[None, :]).astype(f)
    t, q = part // 32, part % 32
    row = np.where(q < Q, QROWS * q + t, -1000)[:, None, None] + ROWS * np.arange(NB)[None, :, None]
    vband = (np.abs(row - np.arange(H)[None, None, :]) <= 2).astype(f)
    band = (np.abs(np.arange(W)[:, None] - np.arange(W)[None, :]) <= 2).astype(f)
    onehot = (np.arange(H)[:, None, None] == QROWS * np.arange(Q)[None, None, :] + np.arange(QROWS)[None, :, None]).astype(f)
    return dict(eye=eye, shift=shift, g96=g96, g96k=g96k, g128=g128, quarter=quarter, vband=vband, band=band,
                onehot=onehot), np.argsort(idx)


def kernel(x, L0_conv_W1, L0_conv_b1, L0_conv_W2, L0_conv_b2):
    import concourse.bacc as bacc
    from concourse.bass_utils import run_bass_kernel_spmd

    tables, reader = constants()
    order = [np.arange(C), reader, np.arange(C), reader]
    w2 = np.asarray(L0_conv_W2).reshape(PARTS, C, SQ)
    b2 = np.asarray(L0_conv_b2).reshape(PARTS, C)
    arrays = {
        "x": np.asarray(x),
        "w1t": np.ascontiguousarray(np.asarray(L0_conv_W1).T),
        "b1": np.asarray(L0_conv_b1).reshape(SQ, 1),
        "w2t": np.ascontiguousarray(np.stack([w2[s][order[s]] for s in range(PARTS)]).transpose(2, 0, 1)),
        "b2": np.ascontiguousarray(np.stack([b2[s][order[s]] for s in range(PARTS)], axis=1)),
        **tables,
    }
    nc = bacc.Bacc("TRN2", target_bir_lowering=False, num_devices=1)
    args = [nc.dram_tensor(f"in_{n}", a.shape, mybir.dt.from_np(a.dtype), kind="ExternalInput").ap()
            for n, a in arrays.items()]
    args.append(nc.dram_tensor("out", (B, C, H, W), mybir.dt.float32, kind="ExternalOutput").ap())
    build(nc, *args)
    r = run_bass_kernel_spmd(nc, [{f"in_{n}": a for n, a in arrays.items()}], core_ids=[0])
    return r.results[0]["out"]
```

```python
from contextlib import ExitStack

import numpy as np
import concourse.bass as bass
from concourse import mybir

B, C, H, W = 32, 96, 112, 112
HW = H * W
GROUPS = 32
J = C // GROUPS
Q = 4
QROWS = H // Q
QN = HW // Q
ROWS = 4
BW = ROWS * W
NB = QN // BW
P = 128
SQ = 24
PARTS = 4
ONES = C
EPS = 1e-5
K_CONST, ALPHA = 2.0, 1e-4
LAG = 1

COEF = ["aggr", "gmean", "spread", "gvar", "nmean", "negk", "veps", "rs", "y", "hid_ps", "hid",
        "mlp_ps", "mlp", "scaled", "coef", "p0", "p1", "i0", "i1", "whole", "crow_ps", "crow"]
NORM = ["gsum", "reduced", "dev", "ndev2", "veps", "rs", "nbias"]
BOX = ["sums", "vert_ps", "vert", "full_ps", "t", "root", "t_root", "root2", "d0",
       "w", "w2", "a", "e", "g", "d", "hi", "lo"]


def build(nc, x, w1t, b1, w2t, b2, eye, shift, g96, dev96, g96k, g128, quarter, vband, band, onehot, out):
    f32, f16, f8 = mybir.dt.float32, mybir.dt.float16, mybir.dt.float8e4
    ALU, ACT = mybir.AluOpType, mybir.ActivationFunctionType
    AX = mybir.AxisListType

    x_v = x.rearrange("n c h w -> n c (h w)").rearrange("n c (q b m) -> n b c q m", q=Q, b=NB)
    out_v = out.rearrange("n c h w -> n c (h w)").rearrange("n (r j) (q b m) -> n b q r j m", j=J, q=Q, b=NB)

    ctx = ExitStack()
    with ctx:
        def sb(name, shape, dt=f32):
            return ctx.enter_context(nc.sbuf_tensor(name, shape, dt))

        def ps(name, shape):
            return ctx.enter_context(nc.psum_tensor(name, shape, f32))

        def sem(name):
            return ctx.enter_context(nc.semaphore(name))

        xin = [sb(f"xin{p}", [P, NB, Q, BW]) for p in range(2)]
        x1 = [sb(f"x1_{p}", [P, NB, J, BW]) for p in range(2)]
        squares = [sb(f"squares{n}", [P, J, BW]) for n in range(3)]
        f1_sb = sb("f1_sb", [P, J, BW])
        s_sb = sb("s_sb", [P, W])
        eye_sb = sb("eye_sb", [C, C], f16)
        shift_sb = sb("shift_sb", [C, C], f16)
        g96_sb = sb("g96_sb", [C, C])
        dev96_sb = sb("dev96_sb", [C, C])
        g96k_sb = sb("g96k_sb", [C, P])
        g128_sb = sb("g128_sb", [P, P])
        quarter_sb = sb("quarter_sb", [P, NB, 32])
        vband_sb = sb("vband_sb", [P, H])
        band_sb = sb("band_sb", [W, W])
        onehot_sb = sb("onehot_sb", [H, QROWS, Q, 32], f8)
        w1t_sb = sb("w1t_sb", [C, SQ])
        w2t_sb = sb("w2t_sb", [SQ, PARTS, C])
        b1_sb = sb("b1_sb", [SQ, 1])
        b2_sb = sb("b2_sb", [C, PARTS])
        minus_half = sb("minus_half", [P, 1])
        onehot_f = s_sb[0:H, :].rearrange("p (o q) -> p o q", q=Q)
        bn = sb("bn", [C, NB * Q, 6])
        mv = sb("mv", [C, 2])
        coef_columns = sb("coef_columns", [C, 5])
        nmean, spread, veps, rs, y = (coef_columns[:, n:n + 1] for n in range(5))
        negk = [sb(f"negk{p}", [P, 1]) for p in range(2)]
        hid = sb("hid", [SQ, 1])
        mlp, scaled, coef = (sb(n, [C, PARTS]) for n in ("mlp", "scaled", "coef"))
        wprime = sb("wprime", [C, 2, C])
        wmix = [sb(f"wmix{p}", [P, 2, J, GROUPS]) for p in range(2)]
        sums = [sb(f"sums{p}", [P, 2, NB]) for p in range(2)]
        me = [sb(f"me{p}", [P, 2]) for p in range(2)]
        dev, ndev2, veps1 = (sb(n, [P, 1]) for n in ("dev", "ndev2", "veps1"))
        rs1 = [sb(f"rs1_{p}", [P, 1]) for p in range(2)]
        nbias = [sb(f"nbias{p}", [P, 1]) for p in range(2)]
        box = {n: sb(f"box_{n}", [H, W]) for n in ("t", "root", "w2", "d0")}
        box |= {"vert": box["t"], "t_root": box["root"], "root2": box["root"], "w": box["root"],
                "a": box["root"], "e": box["w2"], "g": box["root"], "d": box["w2"]}
        d_hi, d_lo = sb("d_hi", [H, W], f16), sb("d_lo", [H, W], f16)

        f1 = ps("f1", [P, J, 512])
        f2 = ps("f2", [P, J, 512])
        shared = ps("shared", [P, 512])
        d_wide = ps("d_wide", [P, 512])

        pool_passed, dve_passed, pe_passed = sem("pool_passed"), sem("dve_passed"), sem("pe_passed")
        consts_in = sem("consts_in")
        rows_set = sem("rows_set")
        ones_set = sem("ones_set")
        onehot_set = sem("onehot_set")
        loaded = [[sem(f"loaded{p}_{b}") for b in range(NB)] for p in range(2)]
        stored = [[sem(f"stored{p}_{b}") for b in range(NB)] for p in range(2)]
        bn_done = sem("bn_done")
        coef_link = sem("coef_link")
        norm_link = sem("norm_link")
        box_link = sem("box_link")
        f1_ready = sem("f1_ready")
        f1_evacuated = sem("f1_evacuated")
        f2_ready = sem("f2_ready")
        x1_ready = sem("x1_ready")
        sumsq_ready = sem("sumsq_ready")
        squares_ready = sem("squares_ready")
        pair_ready = sem("pair_ready")
        group_squares_ready = sem("group_squares_ready")
        chansum_ready = sem("chansum_ready")
        d_ready = sem("d_ready")
        e_ready = sem("e_ready")
        scaled_ready = sem("scaled_ready")
        result_ready = sem("result_ready")

        CONSTS = [(eye_sb, eye), (shift_sb, shift), (g96_sb, g96), (dev96_sb, dev96), (g96k_sb, g96k), (g128_sb, g128),
                  (quarter_sb, quarter), (vband_sb, vband), (band_sb, band), (onehot_f, onehot),
                  (w1t_sb, w1t), (w2t_sb, w2t), (b1_sb, b1), (b2_sb, b2)]

        def count(img, per_image, more):
            k, p = img
            return k * (2 * per_image) + (per_image * p + more)

        def wait(eng, semaphore, img, per_image, more):
            v = count(img, per_image, more)
            if not isinstance(v, int) or v > 0:
                eng.wait_ge(semaphore, v)

        def wait_apart(eng, semaphore, img, per_image, more, passed):
            v = count(img, per_image, more)
            if isinstance(v, int):
                if v > 0:
                    eng.wait_ge(semaphore, v)
            else:
                eng.wait_ge(semaphore, v)
                eng.sem_inc(passed, 1)

        def after(eng, chain, semaphore, img, link):
            wait(eng, semaphore, img, len(chain), chain.index(link) + 1)

        def begins(eng, chain, semaphore, img):
            wait(eng, semaphore, img, len(chain), 0)

        def plus(img, n):
            k, p = img
            return (k + (p + n) // 2, (p + n) % 2)

        def exists(img):
            k, p = img
            return not isinstance(k, int) or 0 <= 2 * k + p < B

        FIRST, LAST = -1, B + 1
        LOOP = (2, B // 2 - 1)

        def iterations(eng, body):
            for n in range(FIRST, 2 * LOOP[0]):
                body((n // 2, n % 2))
            with eng.Fori(*LOOP) as k:
                body((k, 0))
                body((k, 1))
            for n in range(2 * LOOP[1], LAST + 1):
                body((n // 2, n % 2))

        def behind(img, b):
            return (plus(img, -2), b + LAG) if b + LAG < NB else (plus(img, -1), b + LAG - NB)

        def before(img, b):
            return (img, b - 1) if b else (plus(img, -1), NB - 1)

        STATS_AT = {0: 2, 1: 6, 2: 7, 3: 7, 4: 6}
        SQUARES_AT = {0: [0], 1: [1, 2], 2: [3, 4], 3: [5, 6]}

        block = ctx.enter_context(nc.Block())

        @block.sync
        def _(sp):
            def load(img, b):
                wait(sp, f2_ready, plus(img, -2), NB, b + 1)
                k, p = img
                sp.dma_start(xin[p][0:C, b], x_v[2 * k + p, b]).then_inc(loaded[p][b], 16)

            def store(img, b):
                wait(sp, result_ready, img, NB, b + 1)
                k, p = img
                for q in range(Q):
                    sp.dma_start(out_v[2 * k + p, b, q], x1[p][32 * q:32 * q + 32, b]).then_inc(stored[p][b], 16)

            for b in range(2):
                load((0, 0), b)
            for dst, src in CONSTS:
                sp.dma_start(dst[tuple(slice(None) for _ in dst.shape)], src).then_inc(consts_in, 16)
            for b in range(2, NB):
                load((0, 0), b)
            for b in range(NB):
                load((0, 1), b)

            def body(img):
                for b in range(NB):
                    old, ob = behind(img, b)
                    if exists(old):
                        store(old, ob)
                    nxt = plus(img, 2)
                    if exists(img) and exists(nxt):
                        load(nxt, b)

            iterations(sp, body)
            for p in range(2):
                for b in range(NB):
                    sp.wait_ge(stored[p][b], 16 * Q * (B // 2))

        @block.gpsimd
        def _(pool):
            for n in range(2):
                if n:
                    pool.wait_ge(rows_set, n)
                nc.gpsimd.memset(wmix[n][C:P], 0.0).then_inc(rows_set, 1)
            pool.wait_ge(rows_set, 2)
            nc.gpsimd.memset(minus_half[:], -0.5).then_inc(rows_set, 1)
            pool.wait_ge(rows_set, 3)
            for n in range(2):
                if n:
                    pool.wait_ge(ones_set, n)
                nc.gpsimd.memset(xin[n][C:P], 1.0).then_inc(ones_set, 1)
            pool.wait_ge(ones_set, 2)

            def add_squares(img, b):
                first, second, third = (squares[b % 3][:, j] for j in range(J))
                wait(pool, squares_ready, img, NB, b + 1)
                nc.gpsimd.tensor_tensor(first, first, second, ALU.add).then_inc(pair_ready, 1)
                wait(pool, pair_ready, img, NB, b + 1)
                nc.gpsimd.tensor_tensor(first, first, third, ALU.add).then_inc(group_squares_ready, 1)
                wait(pool, group_squares_ready, img, NB, b + 1)

            def newton(img):
                def begin():
                    wait(pool, box_link, img, len(BOX), BOX.index(o))

                for o, a, b in (("w", "t", "d0"), ("w2", "w", "w"), ("a", "w", "d0"), ("e", "w2", "a")):
                    begin()
                    nc.gpsimd.tensor_tensor(box[o][:], box[a][:], box[b][:], ALU.mult).then_inc(box_link, 1)
                o = "g"
                wait_apart(pool, box_link, img, len(BOX), BOX.index(o), pool_passed)
                nc.gpsimd.tensor_scalar(box["g"][:], box["e"][:], -0.25, 1.25, ALU.mult, ALU.add).then_inc(box_link, 1)
                o = "d"
                begin()
                nc.gpsimd.tensor_tensor(box["d"][:], box["d0"][:], box["g"][:], ALU.mult).then_inc(box_link, 1)
                after(pool, BOX, box_link, img, "d")

            def body(img):
                for b in range(NB):
                    old, ob = behind(img, b)
                    prev, nxt = plus(img, -1), plus(img, 1)
                    if exists(old):
                        wait(pool, result_ready, old, NB, ob)
                    if b == 0 and exists(prev):
                        p = prev[1]
                        after(pool, NORM, norm_link, prev, "veps")
                        nc.gpsimd.tensor_tensor(rs1[p][:], veps1[:], minus_half[:], ALU.pow).then_inc(norm_link, 1)
                        after(pool, NORM, norm_link, prev, "rs")
                    if b == 5 and exists(nxt):
                        after(pool, COEF, coef_link, nxt, "veps")
                        nc.gpsimd.tensor_tensor(rs[:], veps[:], minus_half[0:C], ALU.pow).then_inc(coef_link, 1)
                        after(pool, COEF, coef_link, nxt, "rs")
                    if b == 5 and exists(prev):
                        newton(prev)
                    if exists(old):
                        p = old[1]
                        wait_apart(pool, scaled_ready, old, NB, ob + 1, pool_passed)
                        nc.gpsimd.tensor_scalar(x1[p][:, ob], x1[p][:, ob], 1.0, me[p][:, 0:1],
                                                ALU.mult, ALU.add).then_inc(result_ready, 1)
                    if exists(prev) and b in SQUARES_AT:
                        if exists(old):
                            wait(pool, result_ready, old, NB, ob + 1)
                        for i in SQUARES_AT[b]:
                            add_squares(prev, i)

            iterations(pool, body)

        @block.scalar
        def _(act):
            def evacuate(img, b):
                wait(act, sumsq_ready, img, NB, b)
                wait(act, f1_ready, img, NB, b + 1)
                nc.scalar.activation(f1_sb[:], f1[:, :, 0:BW], ACT.Identity).then_inc(f1_evacuated, 1)

            def sum_squares(img, b):
                p = img[1]
                wait(act, x1_ready, img, NB, b + 1)
                if b == 0:
                    after(act, COEF, coef_link, img, "negk")
                nc.scalar.activation(f1_sb[:], x1[p][:, b], ACT.Square, bias=negk[p][:, 0:1],
                                     accum_out=sums[p][:, 1, b:b + 1]).then_inc(sumsq_ready, 1)

            def normalised_squares(img, b):
                p = img[1]
                if b == 0:
                    after(act, NORM, norm_link, img, "nbias")
                wait(act, chansum_ready, img, NB, max(b - 2, 0))
                buf = squares[b % 3]
                nc.scalar.activation(buf[:], x1[p][:, b], ACT.Square, bias=nbias[p][:, 0:1],
                                     scale=rs1[p][:, 0:1]).then_inc(squares_ready, 1)

            def factor(img, b):
                p = img[1]
                wait(act, d_ready, img, NB, b + 1)
                nc.scalar.activation(d_wide[:, 0:BW], d_wide[:, 0:BW], ACT.Identity, bias=1.0,
                                     scale=rs1[p][:, 0:1]).then_inc(e_ready, 1)

            def root(img, src, dst):
                after(act, BOX, box_link, img, src)
                nc.scalar.activation(box[dst][:], box[src][:], ACT.Sqrt).then_inc(box_link, 1)

            def evacuate_sums(img):
                begins(act, BOX, box_link, img)
                wait(act, chansum_ready, img, NB, NB)
                nc.scalar.activation(s_sb[:], shared[:, 0:W], ACT.Identity).then_inc(box_link, 1)

            def box_vert(img):
                after(act, BOX, box_link, img, "vert_ps")
                nc.scalar.activation(box["vert"][:], shared[0:W, 0:H], ACT.Identity).then_inc(box_link, 1)

            def body(img):
                prev = plus(img, -1)
                for b in range(NB):
                    old, ob = behind(img, b)
                    done, db = before(img, b)
                    if exists(old) and ob > 0:
                        factor(old, ob)
                    if exists(done):
                        sum_squares(done, db)
                    if b == 5 and exists(prev):
                        root(prev, "t", "root")
                    if exists(img):
                        evacuate(img, b)
                    if b == 4 and exists(prev):
                        evacuate_sums(prev)
                        box_vert(prev)
                    if b == 5 and exists(prev):
                        root(prev, "t_root", "root2")
                    if exists(old) and ob == 0:
                        factor(old, ob)
                    if exists(prev):
                        for sb_ in SQUARES_AT.get(b, []):
                            normalised_squares(prev, sb_)

            iterations(act, body)

        @block.vector
        def _(dve):
            V = nc.vector

            def statistics(img, first, n):
                k, p = img
                if first == 0:
                    after(dve, COEF, coef_link, plus(img, -1), "aggr")
                for i in range(first, first + n):
                    if i % Q == 0:
                        dve.wait_ge(loaded[p][i // Q], k * 16 + 16)
                    V.bn_stats(bn[:, i], xin[p][0:C, i // Q, i % Q]).then_inc(bn_done, 1)

            def link(chain, semaphore, img, name, ins_of):
                wait(dve, semaphore, img, len(chain), chain.index(name))
                ins_of().then_inc(semaphore, 1)

            def coef_begin(img):
                begins(dve, COEF, coef_link, img)
                wait_apart(dve, bn_done, img, NB * Q, NB * Q, dve_passed)
                V.bn_aggr(mv[:], bn[:]).then_inc(coef_link, 1)

            def coef_centre(img):
                p = img[1]

                def c(name, ins_of):
                    link(COEF, coef_link, img, name, ins_of)

                c("spread", lambda: V.scalar_tensor_tensor(out=spread[:], in0=shared[0:C, 8:9],
                                                           scalar=shared[0:C, 8:9], in1=mv[:, 1:2],
                                                           op0=ALU.mult, op1=ALU.add))
                c("nmean", lambda: V.tensor_scalar(nmean[:], shared[0:C, 0:1], -1.0, None, ALU.mult))
                c("negk", lambda: V.tensor_scalar(negk[p][:], shared[:, 1:2], -1.0, None, ALU.mult))

            def coef_y(img):
                def c(name, ins_of):
                    link(COEF, coef_link, img, name, ins_of)

                c("veps", lambda: V.tensor_scalar(veps[:], shared[0:C, 2:3], EPS, None, ALU.add))

                c("y", lambda: V.tensor_scalar(y[:], shared[0:C, 8:9], rs[:, 0:1], None, ALU.mult))

            def coef_hid(img):
                def c(name, ins_of):
                    link(COEF, coef_link, img, name, ins_of)

                c("hid", lambda: V.tensor_scalar(hid[:], shared[0:SQ, 3:4], b1_sb[:, 0:1], 0.0, ALU.add, ALU.max))

            def coef_end(img):
                p = img[1]

                def c(name, ins_of):
                    link(COEF, coef_link, img, name, ins_of)

                c("mlp", lambda: V.tensor_tensor(mlp[:], shared[0:C, 4:4 + PARTS], b2_sb[:], ALU.add))
                c("scaled", lambda: V.tensor_scalar(scaled[:], mlp[:], 2.0 / 3.0, -2.0, ALU.mult, ALU.max))
                c("coef", lambda: V.tensor_scalar(coef[:], scaled[:], 2.0, rs[:, 0:1], ALU.min, ALU.mult))

                for i in range(2):
                    c(f"p{i}", lambda: V.tensor_scalar(wprime[:, i], shift_sb[:], coef[:, 2 * i + 1:2 * i + 2],
                                                       None, ALU.mult))
                for i in range(2):
                    c(f"i{i}", lambda: V.scalar_tensor_tensor(
                        out=wprime[:, i], in0=eye_sb[:], scalar=coef[:, 2 * i:2 * i + 1], in1=wprime[:, i],
                        op0=ALU.mult, op1=ALU.add))
                wait(dve, f2_ready, plus(img, -1), NB, 0)
                c("whole", lambda: V.tensor_tensor(
                    wmix[p][0:C].rearrange("k i j r -> k i (j r)"), wprime[:],
                    eye_sb[:, None, :].to_broadcast([C, 2, C]), ALU.add))

            def coef_row(img):
                p = img[1]

                def c(name, ins_of):
                    link(COEF, coef_link, img, name, ins_of)

                c("crow", lambda: V.tensor_copy(wmix[p][ONES:ONES + 1].rearrange("k i j r -> k (i j r)"),
                                                shared[ONES:ONES + 1, 64:64 + 2 * C]))

            def maximum(img, b):
                p = img[1]
                if not isinstance(img[0], int) or img[0] > 0:
                    dve.wait_ge(stored[p][b], img[0] * (16 * Q))
                wait(dve, f1_evacuated, img, NB, b + 1)
                wait(dve, f2_ready, img, NB, b + 1)
                V.scalar_tensor_tensor(out=x1[p][:, b], in0=f2[:, :, 0:BW], scalar=0.0, in1=f1_sb[:],
                                       op0=ALU.add, op1=ALU.max,
                                       accum_out=sums[p][:, 0, b:b + 1]).then_inc(x1_ready, 1)

            def norm(img):
                p = img[1]

                def c(name, ins_of):
                    link(NORM, norm_link, img, name, ins_of)

                c("reduced", lambda: V.tensor_reduce(
                    me[p][:], shared[:, 256:256 + 2 * NB].rearrange("p (s b) -> p s b", s=2), AX.X, ALU.add))
                c("dev", lambda: V.tensor_scalar(dev[:], me[p][:, 0:1], negk[p][:, 0:1], None, ALU.add))
                c("ndev2", lambda: V.tensor_scalar(ndev2[:], dev[:], dev[:, 0:1], -1.0, ALU.mult, ALU.mult))
                c("veps", lambda: V.scalar_tensor_tensor(out=veps1[:], in0=me[p][:, 1:2], scalar=EPS, in1=ndev2[:],
                                                         op0=ALU.add, op1=ALU.add))
                c("nbias", lambda: V.tensor_scalar(nbias[p][:], me[p][:, 0:1], rs1[p][:, 0:1], -1.0,
                                                   ALU.mult, ALU.mult))

            def box_step(img, name, ins_of):
                link(BOX, box_link, img, name, ins_of)

            def box_t(img):
                box_step(img, "t", lambda: V.tensor_scalar(box["t"][:], shared[0:H, 128:128 + W], ALPHA, K_CONST,
                                                           ALU.mult, ALU.add))

            def box_t_root(img):
                box_step(img, "t_root", lambda: V.tensor_tensor(box["t_root"][:], box["t"][:], box["root"][:], ALU.mult))

            def box_power(img):
                box_step(img, "d0", lambda: V.reciprocal(box["d0"][:], box["root2"][:]))

            def box_halves(img):
                wait(dve, d_ready, img, NB, 0)
                box_step(img, "hi", lambda: V.tensor_copy(d_hi[:], box["d"][:]))
                box_step(img, "lo", lambda: V.tensor_tensor(d_lo[:], box["d"][:], d_hi[:], ALU.subtract))

            def scale(img, b):
                p = img[1]
                wait(dve, e_ready, img, NB, b + 1)
                V.scalar_tensor_tensor(out=x1[p][:, b], in0=x1[p][:, b], scalar=me[p][:, 0:1],
                                       in1=d_wide[:, None, 0:BW].to_broadcast([P, J, BW]),
                                       op0=ALU.subtract, op1=ALU.mult).then_inc(scaled_ready, 1)

            dve.wait_ge(consts_in, 16 * len(CONSTS))
            V.tensor_copy(onehot_sb[:], onehot_f[:, :, :, None].to_broadcast([H, QROWS, Q, 32]),
                          saturate=False).then_inc(onehot_set, 1)
            dve.wait_ge(rows_set, 3)

            def body(img):
                prev, nxt = plus(img, -1), plus(img, 1)
                for b in range(NB):
                    old, ob = behind(img, b)
                    done, db = before(img, b)
                    if b == 6 and exists(nxt):
                        coef_hid(nxt)
                    if exists(done):
                        maximum(done, db)
                    if b == 5 and exists(prev):
                        box_t(prev)
                    if b == 6 and exists(prev):
                        box_halves(prev)
                    if b == 6 and exists(nxt):
                        coef_end(nxt)
                        coef_row(nxt)
                    if exists(old):
                        scale(old, ob)
                    if b == 0 and exists(prev):
                        norm(prev)
                    if b == 5 and exists(nxt):
                        coef_centre(nxt)
                    if b == 5 and exists(prev):
                        box_t_root(prev)
                    if b == 5 and exists(nxt):
                        coef_y(nxt)
                    if b == 5 and exists(prev):
                        box_power(prev)
                    if exists(nxt) and b in STATS_AT:
                        statistics(nxt, sum(STATS_AT[i] for i in range(b)), STATS_AT[b])
                    if b == 4 and exists(nxt):
                        coef_begin(nxt)

            iterations(dve, body)

        @block.tensor
        def _(pe):
            T = nc.tensor

            def mix(img, b, i, j):
                p = img[1]
                if j == 0:
                    if b == 0 and i == 0:
                        after(pe, COEF, coef_link, img, "crow")
                        if isinstance(img[0], int) and img == (0, 1):
                            pe.wait_ge(ones_set, 2)
                    wait(pe, (f1_evacuated, x1_ready)[i], img, NB, b)
                dst = (f1, f2)[i]
                for q in range(Q):
                    last = T.matmul(dst[32 * q:32 * q + 32, j, 0:BW], wmix[p][:, i, j, :], xin[p][:, b, q, :],
                                    start=True, stop=True)
                if j == J - 1:
                    last.then_inc((f1_ready, f2_ready)[i], 1)

            def coef_groups(img):
                after(pe, BOX, box_link, plus(img, -2), "t")
                after(pe, COEF, coef_link, img, "aggr")
                T.matmul(shared[0:C, 8:9], dev96_sb[:], mv[:, 0:1], start=True, stop=True)
                T.matmul(shared[0:C, 0:1], g96_sb[:], mv[:, 0:1], start=True, stop=True)
                T.matmul(shared[:, 1:2], g96k_sb[:], mv[:, 0:1], start=True, stop=True).then_inc(coef_link, 1)

            def coef_var(img):
                after(pe, COEF, coef_link, img, "spread")
                T.matmul(shared[0:C, 2:3], g96_sb[:], spread[:], start=True, stop=True).then_inc(coef_link, 1)

            def coef_y(img):
                after(pe, COEF, coef_link, img, "y")
                T.matmul(shared[0:SQ, 3:4], w1t_sb[:], y[:], start=True, stop=True).then_inc(coef_link, 1)

            def coef_mlp(img):
                after(pe, COEF, coef_link, img, "hid")
                for s in range(PARTS):
                    last = T.matmul(shared[0:C, 4 + s:5 + s], w2t_sb[:, s, :], hid[:], start=True, stop=True)
                last.then_inc(coef_link, 1)

            def coef_row(img):
                after(pe, COEF, coef_link, img, "whole")
                T.matmul(shared[ONES:ONES + 1, 64:64 + 2 * C], nmean[:], wprime[:].rearrange("k i c -> k (i c)"),
                         start=True, stop=True).then_inc(coef_link, 1)

            def group_sums(img):
                wait(pe, x1_ready, img, NB, NB)
                wait(pe, sumsq_ready, img, NB, NB)
                begins(pe, NORM, norm_link, img)
                T.matmul(shared[:, 256:256 + 2 * NB], g128_sb[:], sums[img[1]][:].rearrange("p s b -> p (s b)"),
                         start=True, stop=True).then_inc(norm_link, 1)

            def channel_sum(img, b):
                wait(pe, group_squares_ready, img, NB, b + 1)
                for t in range(ROWS):
                    last = T.matmul(shared[32 * t:32 * t + 32, 0:W], quarter_sb[:, b, :],
                                    squares[b % 3][:, 0, t * W:t * W + W], start=(b == 0), stop=(b == NB - 1))
                last.then_inc(chansum_ready, 1)

            def box_vert(img):
                after(pe, BOX, box_link, img, "sums")
                T.matmul(shared[0:W, 0:H], s_sb[:], vband_sb[:], start=True, stop=True).then_inc(box_link, 1)

            def box_full(img):
                after(pe, BOX, box_link, img, "vert")
                T.matmul(shared[0:H, 128:128 + W], box["vert"][:], band_sb[:], start=True, stop=True).then_inc(box_link, 1)

            def spread_d(img, b):
                if b == 0:
                    after(pe, BOX, box_link, img, "lo")
                wait_apart(pe, scaled_ready, img, NB, b, pe_passed)
                for t in range(ROWS):
                    rows = onehot_sb[:, ROWS * b + t].rearrange("h q r -> h (q r)")
                    for half in (d_hi, d_lo):
                        last = T.matmul(d_wide[:, t * W:t * W + W], rows, half[:], start=(half is d_hi),
                                        stop=(half is d_lo))
                last.then_inc(d_ready, 1)

            pe.wait_ge(consts_in, 16 * len(CONSTS))
            pe.wait_ge(onehot_set, 1)
            pe.wait_ge(ones_set, 1)

            BETWEEN = {(0, 4): [(group_sums, -1)], (2, 3): [(channel_sum, -1, 0)], (2, 5): [(channel_sum, -1, 1)],
                       (3, 1): [(channel_sum, -1, 2)], (3, 4): [(channel_sum, -1, 3)],
                       (4, 4): [(channel_sum, -1, 4), (channel_sum, -1, 5)], (5, 0): [(channel_sum, -1, 6)],
                       (5, 1): [(box_vert, -1)], (5, 2): [(box_full, -1)], (5, 3): [(coef_groups, 1), (coef_var, 1)],
                       (6, 0): [(coef_y, 1)], (6, 1): [(coef_mlp, 1)], (6, 5): [(coef_row, 1)]}
            SPREAD_AT = 1, 3

            def body(img):
                for b in range(NB):
                    old, ob = behind(img, b)
                    for part in range(2 * J):
                        for what, n, *args in BETWEEN.get((b, part), []):
                            if exists(plus(img, n)):
                                what(plus(img, n), *args)
                        if exists(old) and part == SPREAD_AT[ob == 0]:
                            spread_d(old, ob)
                        if exists(img):
                            mix(img, b, part // J, part % J)

            iterations(pe, body)


def constants():
    cg = C // 6
    idx = np.arange(C).reshape(6, cg)
    idx = np.concatenate([idx[1:], idx[:1]], axis=0)
    idx = np.concatenate([idx[:, 1:], idx[:, :1]], axis=1).reshape(C)
    chan = np.array([J * r + j for j in range(J) for r in range(GROUPS)])
    f = np.float32
    k = np.arange(C)[:, None]
    eye = (k == chan[None, :]).astype(np.float16)
    shift = (k == idx[chan][None, :]).astype(np.float16)
    g96 = (k // J == k.T // J).astype(f) / f(J)
    dev96 = np.eye(C, dtype=f) - g96
    part = np.arange(P)
    g96k = (k // J == part[None, :] % GROUPS).astype(f) / f(J)
    g128 = (part[:, None] % GROUPS == part[None, :] % GROUPS).astype(f) / f(J * HW)
    col = np.arange(32)
    quarter = ((col[None, None, :] // Q == np.arange(NB)[None, :, None])
               & (col[None, None, :] % Q == part[:, None, None] // GROUPS)).astype(f)
    t, b, q = part // 32, part % 32 // Q, part % Q
    row = np.where(b < NB, QROWS * q + ROWS * b + t, -1000)
    vband = (np.abs(row[:, None] - np.arange(H)[None, :]) <= 2).astype(f)
    band = (np.abs(np.arange(W)[:, None] - np.arange(W)[None, :]) <= 2).astype(f)
    onehot = (np.arange(H)[:, None, None] == QROWS * np.arange(Q)[None, None, :] + np.arange(QROWS)[None, :, None]).astype(f)
    return dict(eye=eye, shift=shift, g96=g96, dev96=dev96, g96k=g96k, g128=g128, quarter=quarter, vband=vband, band=band,
                onehot=onehot), np.argsort(idx)


def kernel(x, L0_conv_W1, L0_conv_b1, L0_conv_W2, L0_conv_b2):
    import concourse.bacc as bacc
    from concourse.bass_utils import run_bass_kernel_spmd

    tables, reader = constants()
    order = [np.arange(C), reader, np.arange(C), reader]
    w2 = np.asarray(L0_conv_W2).reshape(PARTS, C, SQ)
    b2 = np.asarray(L0_conv_b2).reshape(PARTS, C)
    arrays = {
        "x": np.asarray(x),
        "w1t": np.ascontiguousarray(np.asarray(L0_conv_W1).T),
        "b1": np.asarray(L0_conv_b1).reshape(SQ, 1),
        "w2t": np.ascontiguousarray(np.stack([w2[s][order[s]] for s in range(PARTS)]).transpose(2, 0, 1)),
        "b2": np.ascontiguousarray(np.stack([b2[s][order[s]] for s in range(PARTS)], axis=1)),
        **tables,
    }
    nc = bacc.Bacc("TRN2", target_bir_lowering=False, num_devices=1)
    args = [nc.dram_tensor(f"in_{n}", a.shape, mybir.dt.from_np(a.dtype), kind="ExternalInput").ap()
            for n, a in arrays.items()]
    args.append(nc.dram_tensor("out", (B, C, H, W), mybir.dt.float32, kind="ExternalOutput").ap())
    build(nc, *args)
    r = run_bass_kernel_spmd(nc, [{f"in_{n}": a for n, a in arrays.items()}], core_ids=[0])
    return r.results[0]["out"]
```

```python
from contextlib import ExitStack
from itertools import islice

import numpy as np
import concourse.bass as bass
from concourse import mybir

B, C, H, W = 32, 96, 112, 112
HW = H * W
GROUPS = 32
J = C // GROUPS
Q = 4
QROWS = H // Q
QN = HW // Q
ROWS = 4
BW = ROWS * W
NB = QN // BW
P = 128
SQ = 24
PARTS = 4
ONES = C
EPS = 1e-5
K_CONST, ALPHA = 2.0, 1e-4
LAG = 1

COEF = ["aggr", "gmean", "spread", "gvar", "nmean", "negk", "veps", "rs", "y", "hid_ps", "hid",
        "mlp", "scaled", "coef", "p0", "p1", "i0", "i1", "crow_ps", "crow"]
NORM = ["gsum", "reduced", "dev", "ndev2", "veps", "rs", "nbias"]
BOX = ["sums", "vert_ps", "vert", "full_ps", "t", "root", "t_root", "root2", "d0",
       "w", "w2", "a", "e", "g", "d", "hi", "lo"]


def build(nc, x, w1t, b1, w2t, eye, neg_eye, shift, g96, dev96, g96k, g128, quarter, vband, band, onehot, out):
    f32, f16, f8 = mybir.dt.float32, mybir.dt.float16, mybir.dt.float8e4
    ALU, ACT = mybir.AluOpType, mybir.ActivationFunctionType
    AX = mybir.AxisListType

    x_v = x.rearrange("n c h w -> n c (h w)").rearrange("n c (q b m) -> n b c q m", q=Q, b=NB)
    out_v = out.rearrange("n c h w -> n c (h w)").rearrange("n (r j) (q b m) -> n b q r j m", j=J, q=Q, b=NB)

    ctx = ExitStack()
    with ctx:
        def sb(name, shape, dt=f32):
            return ctx.enter_context(nc.sbuf_tensor(name, shape, dt))

        def ps(name, shape):
            return ctx.enter_context(nc.psum_tensor(name, shape, f32))

        def sem(name):
            return ctx.enter_context(nc.semaphore(name))

        xin = [sb(f"xin{p}", [P, NB, Q, BW]) for p in range(2)]
        x1 = [sb(f"x1_{p}", [P, NB, J, BW]) for p in range(2)]
        squares = [sb(f"squares{n}", [P, J, BW]) for n in range(3)]
        f1_sb = sb("f1_sb", [P, J, BW])
        s_sb = sb("s_sb", [P, W])
        eye_sb = sb("eye_sb", [C, C], f16)
        neg_eye_sb = sb("neg_eye_sb", [C, C])
        shift_sb = sb("shift_sb", [C, C], f16)
        g96_sb = sb("g96_sb", [C, C])
        dev96_sb = sb("dev96_sb", [C, C])
        g96k_sb = sb("g96k_sb", [C, P])
        g128_sb = sb("g128_sb", [P, P])
        quarter_sb = sb("quarter_sb", [P, NB, 32])
        vband_sb = sb("vband_sb", [P, H])
        band_sb = sb("band_sb", [W, W])
        onehot_sb = sb("onehot_sb", [H, QROWS, Q, 32], f8)
        w1t_sb = sb("w1t_sb", [C, SQ])
        w2t_sb = sb("w2t_sb", [SQ + 1, PARTS, C])
        b1_sb = sb("b1_sb", [SQ, 1])
        minus_half = sb("minus_half", [P, 1])
        onehot_f = s_sb[0:H, :].rearrange("p (o q) -> p o q", q=Q)
        bn = sb("bn", [C, NB * Q, 6])
        mv = sb("mv", [C, 2])
        coef_columns = sb("coef_columns", [C, 5])
        nmean, spread, veps, rs, y = (coef_columns[:, n:n + 1] for n in range(5))
        negk = [sb(f"negk{p}", [P, 1]) for p in range(2)]
        hid = sb("hid", [SQ + 1, 1])
        scaled, coef = (sb(n, [C, PARTS]) for n in ("scaled", "coef"))
        wmix = [sb(f"wmix{p}", [P, 2, J, GROUPS]) for p in range(2)]
        sums = [sb(f"sums{p}", [P, 2, NB]) for p in range(2)]
        me = [sb(f"me{p}", [P, 2]) for p in range(2)]
        dev, ndev2, veps1 = (sb(n, [P, 1]) for n in ("dev", "ndev2", "veps1"))
        rs1 = [sb(f"rs1_{p}", [P, 1]) for p in range(2)]
        nbias = [sb(f"nbias{p}", [P, 1]) for p in range(2)]
        box = {n: sb(f"box_{n}", [H, W]) for n in ("t", "root", "w2", "d0")}
        box |= {"vert": box["t"], "t_root": box["root"], "root2": box["root"], "w": box["root"],
                "a": box["root"], "e": box["w2"], "g": box["root"], "d": box["w2"]}
        d_hi, d_lo = sb("d_hi", [H, W], f16), sb("d_lo", [H, W], f16)

        f1 = ps("f1", [P, J, 512])
        f2 = ps("f2", [P, J, 512])
        shared = ps("shared", [P, 512])
        d_wide = ps("d_wide", [P, 512])

        pool_passed, dve_passed, pe_passed = sem("pool_passed"), sem("dve_passed"), sem("pe_passed")
        consts_in = sem("consts_in")
        rows_set = sem("rows_set")
        ones_set = sem("ones_set")
        onehot_set = sem("onehot_set")
        loaded = [[sem(f"loaded{p}_{b}") for b in range(NB)] for p in range(2)]
        stored = [[sem(f"stored{p}_{b}") for b in range(NB)] for p in range(2)]
        bn_done = sem("bn_done")
        coef_link = sem("coef_link")
        norm_link = sem("norm_link")
        box_link = sem("box_link")
        f1_ready = sem("f1_ready")
        f1_evacuated = sem("f1_evacuated")
        f2_ready = sem("f2_ready")
        x1_ready = sem("x1_ready")
        sumsq_ready = sem("sumsq_ready")
        squares_ready = sem("squares_ready")
        pair_ready = sem("pair_ready")
        group_squares_ready = sem("group_squares_ready")
        chansum_ready = sem("chansum_ready")
        d_ready = sem("d_ready")
        e_ready = sem("e_ready")
        scaled_ready = sem("scaled_ready")
        result_ready = sem("result_ready")

        CONSTS = [(eye_sb, eye), (neg_eye_sb, neg_eye), (shift_sb, shift), (g96_sb, g96), (dev96_sb, dev96), (g96k_sb, g96k), (g128_sb, g128),
                  (quarter_sb, quarter), (vband_sb, vband), (band_sb, band), (onehot_f, onehot),
                  (w1t_sb, w1t), (w2t_sb, w2t), (b1_sb, b1)]

        def count(img, per_image, more):
            k, p = img
            return k * (2 * per_image) + (per_image * p + more)

        def wait(eng, semaphore, img, per_image, more):
            v = count(img, per_image, more)
            if not isinstance(v, int) or v > 0:
                eng.wait_ge(semaphore, v)

        def wait_apart(eng, semaphore, img, per_image, more, passed):
            v = count(img, per_image, more)
            if isinstance(v, int):
                if v > 0:
                    eng.wait_ge(semaphore, v)
            else:
                eng.wait_ge(semaphore, v)
                eng.sem_inc(passed, 1)

        def after(eng, chain, semaphore, img, link):
            wait(eng, semaphore, img, len(chain), chain.index(link) + 1)

        def begins(eng, chain, semaphore, img):
            wait(eng, semaphore, img, len(chain), 0)

        def plus(img, n):
            k, p = img
            return (k + (p + n) // 2, (p + n) % 2)

        def exists(img):
            k, p = img
            return not isinstance(k, int) or 0 <= 2 * k + p < B

        def is_last(img):
            k, p = img
            return isinstance(k, int) and 2 * k + p == B - 1

        def d_buffer(img, b):
            return f1[:, 0] if is_last(img) and b % 2 else d_wide

        FIRST, LAST = -1, B + 1
        LOOP = (2, B // 2 - 2, 2)

        def iterations(eng, body):
            for n in range(FIRST, 2 * LOOP[0]):
                body((n // 2, n % 2))
            with eng.Fori(*LOOP) as k:
                for pair in range(2):
                    body((k + pair, 0))
                    body((k + pair, 1))
            for n in range(2 * LOOP[1], LAST + 1):
                body((n // 2, n % 2))

        def behind(img, b):
            return (plus(img, -2), b + LAG) if b + LAG < NB else (plus(img, -1), b + LAG - NB)

        def before(img, b):
            return (img, b - 1) if b else (plus(img, -1), NB - 1)

        PE_PLAN = [
            "mix spread mix mix mix group_sums mix mix",
            "spread mix mix mix mix mix mix",
            "mix mix channel_sum spread mix mix channel_sum mix mix",
            "spread mix mix mix channel_sum mix mix mix",
            "channel_sum mix spread mix channel_sum mix mix channel_sum mix mix",
            "spread channel_sum mix box_vert box_full mix coef_groups mix coef_var mix mix mix",
            "coef_y mix coef_mlp mix mix mix spread coef_row mix mix"]
        DVE_PLAN = [
            "maximum scale norm_moments statistics norm_bias",
            "maximum statistics statistics scale statistics statistics statistics statistics",
            "maximum statistics statistics scale statistics",
            "statistics statistics maximum statistics statistics scale statistics",
            "statistics statistics maximum statistics scale statistics statistics statistics statistics",
            "coef_begin maximum box_t scale box_t_root coef_centre coef_veps box_power statistics statistics coef_y",
            "statistics coef_hid maximum box_halves statistics coef_end statistics coef_row scale statistics"]
        ACT_PLAN = [
            "factor sum_squares evacuate squares",
            "factor sum_squares evacuate squares squares",
            "factor sum_squares evacuate",
            "squares squares factor sum_squares evacuate squares",
            "factor squares sum_squares evacuate",
            "box_sums factor box_vert box_root sum_squares box_root2 evacuate",
            "sum_squares evacuate factor"]
        POOL_PLAN = [
            "norm_rs add_mean add_squares",
            "add_mean add_squares add_squares",
            "add_mean",
            "add_squares add_squares add_mean",
            "add_squares add_squares add_mean",
            "coef_rs newton add_mean",
            "add_mean"]

        def numbered(plan):
            seen = {}
            for b, step in enumerate(plan):
                for name in step.split():
                    yield b, name, seen.get(name, 0)
                    seen[name] = seen.get(name, 0) + 1

        plan = " ".join(DVE_PLAN).split()
        EARLY = plan[plan.index("coef_begin"):].count("statistics")

        block = ctx.enter_context(nc.Block())

        @block.sync
        def _(sp):
            def load(img, b):
                wait(sp, f2_ready, plus(img, -2), NB, b + 1)
                k, p = img
                sp.dma_start(xin[p][0:C, b], x_v[2 * k + p, b]).then_inc(loaded[p][b], 16)

            def store(img, b):
                wait(sp, result_ready, img, NB, b + 1)
                k, p = img
                sp.dma_start(out_v[2 * k + p, b], x1[p][:, b]).then_inc(stored[p][b], 16)

            consts = iter(CONSTS)
            for b in range(NB):
                load((0, 0), b)
                for dst, src in islice(consts, 3 if b > 1 else 0):
                    sp.dma_start(dst[tuple(slice(None) for _ in dst.shape)], src).then_inc(consts_in, 16)
            for b in range(NB):
                load((0, 1), b)

            def body(img):
                for b in range(NB):
                    old, ob = behind(img, b)
                    if exists(old):
                        store(old, ob)
                    nxt = plus(img, 2)
                    if exists(img) and exists(nxt):
                        load(nxt, b)

            iterations(sp, body)
            for p in range(2):
                for b in range(NB):
                    sp.wait_ge(stored[p][b], 16 * (B // 2))

        @block.gpsimd
        def _(pool):
            for n in range(2):
                if n:
                    pool.wait_ge(rows_set, n)
                nc.gpsimd.memset(wmix[n][C:P], 0.0).then_inc(rows_set, 1)
            pool.wait_ge(rows_set, 2)
            nc.gpsimd.memset(minus_half[:], -0.5).then_inc(rows_set, 1)
            pool.wait_ge(rows_set, 3)
            nc.gpsimd.memset(hid[:], 1.0).then_inc(rows_set, 1)
            pool.wait_ge(rows_set, 4)
            for n in range(2):
                if n:
                    pool.wait_ge(ones_set, n)
                nc.gpsimd.memset(xin[n][C:P], 1.0).then_inc(ones_set, 1)
            pool.wait_ge(ones_set, 2)

            def add_squares(img, b):
                first, second, third = (squares[b % 3][:, j] for j in range(J))
                wait(pool, squares_ready, img, NB, b + 1)
                nc.gpsimd.tensor_tensor(first, first, second, ALU.add).then_inc(pair_ready, 1)
                wait(pool, pair_ready, img, NB, b + 1)
                nc.gpsimd.tensor_tensor(first, first, third, ALU.add).then_inc(group_squares_ready, 1)
                wait(pool, group_squares_ready, img, NB, b + 1)

            def newton(img):
                def begin():
                    wait(pool, box_link, img, len(BOX), BOX.index(o))

                for o, a, b in (("w", "t", "d0"), ("w2", "w", "w"), ("a", "w", "d0"), ("e", "w2", "a")):
                    begin()
                    nc.gpsimd.tensor_tensor(box[o][:], box[a][:], box[b][:], ALU.mult).then_inc(box_link, 1)
                o = "g"
                wait_apart(pool, box_link, img, len(BOX), BOX.index(o), pool_passed)
                nc.gpsimd.tensor_scalar(box["g"][:], box["e"][:], -0.25, 1.25, ALU.mult, ALU.add).then_inc(box_link, 1)
                o = "d"
                begin()
                nc.gpsimd.tensor_tensor(box["d"][:], box["d0"][:], box["g"][:], ALU.mult).then_inc(box_link, 1)
                after(pool, BOX, box_link, img, "d")

            def norm_rs(img):
                p = img[1]
                after(pool, NORM, norm_link, img, "veps")
                nc.gpsimd.tensor_tensor(rs1[p][:], veps1[:], minus_half[:], ALU.pow).then_inc(norm_link, 1)
                after(pool, NORM, norm_link, img, "rs")

            def coef_rs(img):
                after(pool, COEF, coef_link, img, "veps")
                nc.gpsimd.tensor_tensor(rs[:], veps[:], minus_half[0:C], ALU.pow).then_inc(coef_link, 1)
                after(pool, COEF, coef_link, img, "rs")

            def add_mean(img, b):
                p = img[1]
                wait_apart(pool, scaled_ready, img, NB, b + 1, pool_passed)
                nc.gpsimd.tensor_scalar(x1[p][:, b], x1[p][:, b], 1.0, me[p][:, 0:1],
                                        ALU.mult, ALU.add).then_inc(result_ready, 1)
                wait(pool, result_ready, img, NB, b + 1)

            def body(img):
                prev, nxt = plus(img, -1), plus(img, 1)
                for b, name, i in numbered(POOL_PLAN):
                    what, which, *args = {
                        "norm_rs": (norm_rs, prev), "coef_rs": (coef_rs, nxt), "newton": (newton, prev),
                        "add_mean": (add_mean, *behind(img, b)), "add_squares": (add_squares, prev, i)}[name]
                    if exists(which) and not (name == "add_squares" and is_last(which)):
                        what(which, *args)

            iterations(pool, body)

        @block.scalar
        def _(act):
            def evacuate(img, b):
                wait(act, sumsq_ready, img, NB, b)
                wait(act, f1_ready, img, NB, b + 1)
                nc.scalar.activation(f1_sb[:], f1[:, :, 0:BW], ACT.Identity).then_inc(f1_evacuated, 1)

            def sum_squares(img, b):
                p = img[1]
                wait(act, x1_ready, img, NB, b + 1)
                if b == 0:
                    after(act, COEF, coef_link, img, "negk")
                nc.scalar.activation(f1_sb[:], x1[p][:, b], ACT.Square, bias=negk[p][:, 0:1],
                                     accum_out=sums[p][:, 1, b:b + 1]).then_inc(sumsq_ready, 1)

            def normalised_squares(img, b):
                p = img[1]
                if b == 0:
                    after(act, NORM, norm_link, img, "nbias")
                wait(act, chansum_ready, img, NB, max(b - 2, 0))
                buf = squares[b % 3]
                nc.scalar.activation(buf[:], x1[p][:, b], ACT.Square, bias=nbias[p][:, 0:1],
                                     scale=rs1[p][:, 0:1]).then_inc(squares_ready, 1)

            def factor(img, b):
                p = img[1]
                wait(act, d_ready, img, NB, b + 1)
                d = d_buffer(img, b)
                nc.scalar.activation(d[:, 0:BW], d[:, 0:BW], ACT.Identity, bias=1.0,
                                     scale=rs1[p][:, 0:1]).then_inc(e_ready, 1)

            def root(img, src, dst):
                after(act, BOX, box_link, img, src)
                nc.scalar.activation(box[dst][:], box[src][:], ACT.Sqrt).then_inc(box_link, 1)

            def box_sums(img):
                begins(act, BOX, box_link, img)
                wait(act, chansum_ready, img, NB, NB)
                nc.scalar.activation(s_sb[:], shared[:, 0:W], ACT.Identity).then_inc(box_link, 1)

            def box_vert(img):
                after(act, BOX, box_link, img, "vert_ps")
                nc.scalar.activation(box["vert"][:], shared[0:W, 0:H], ACT.Identity).then_inc(box_link, 1)

            def body(img):
                prev = plus(img, -1)
                for b, name, i in numbered(ACT_PLAN):
                    what, which, *args = {
                        "factor": (factor, *behind(img, b)), "sum_squares": (sum_squares, *before(img, b)),
                        "evacuate": (evacuate, img, b), "squares": (normalised_squares, prev, i),
                        "box_sums": (box_sums, prev), "box_vert": (box_vert, prev),
                        "box_root": (root, prev, "t", "root"), "box_root2": (root, prev, "t_root", "root2")}[name]
                    if exists(which):
                        what(which, *args)

            iterations(act, body)

        @block.vector
        def _(dve):
            V = nc.vector

            def statistics(img, i):
                k, p = img
                if i == 0:
                    after(dve, COEF, coef_link, plus(img, -1), "aggr")
                if i % Q == 0:
                    dve.wait_ge(loaded[p][i // Q], k * 16 + 16)
                V.bn_stats(bn[:, i], xin[p][0:C, i // Q, i % Q]).then_inc(bn_done, 1)

            def link(chain, semaphore, img, name, ins_of, needs=None):
                wait(dve, semaphore, img, len(chain), chain.index(needs) + 1 if needs else chain.index(name))
                ins_of().then_inc(semaphore, 1)

            def coef_begin(img):
                begins(dve, COEF, coef_link, img)
                wait_apart(dve, bn_done, img, NB * Q, NB * Q, dve_passed)
                V.bn_aggr(mv[:], bn[:]).then_inc(coef_link, 1)

            def coef_centre(img):
                p = img[1]

                def c(name, ins_of, needs=None):
                    link(COEF, coef_link, img, name, ins_of, needs)

                c("spread", lambda: V.scalar_tensor_tensor(out=spread[:], in0=shared[0:C, 8:9],
                                                           scalar=shared[0:C, 8:9], in1=mv[:, 1:2],
                                                           op0=ALU.mult, op1=ALU.add))
                c("nmean", lambda: V.tensor_scalar(nmean[:], shared[0:C, 0:1], -1.0, None, ALU.mult))
                c("negk", lambda: V.tensor_scalar(negk[p][:], shared[:, 1:2], -1.0, None, ALU.mult), "gvar")

            def coef_veps(img):
                def c(name, ins_of, needs=None):
                    link(COEF, coef_link, img, name, ins_of, needs)

                c("veps", lambda: V.tensor_scalar(veps[:], shared[0:C, 2:3], EPS, None, ALU.add))

            def coef_y(img):
                def c(name, ins_of, needs=None):
                    link(COEF, coef_link, img, name, ins_of, needs)

                c("y", lambda: V.tensor_scalar(y[:], shared[0:C, 8:9], rs[:, 0:1], None, ALU.mult))

            def coef_hid(img):
                if isinstance(img[0], int) and img == (0, 0):
                    dve.wait_ge(rows_set, 4)

                def c(name, ins_of, needs=None):
                    link(COEF, coef_link, img, name, ins_of, needs)

                c("hid", lambda: V.tensor_scalar(hid[0:SQ], shared[0:SQ, 3:4], b1_sb[:, 0:1], 0.0, ALU.add, ALU.max))

            def coef_end(img):
                p = img[1]

                def c(name, ins_of, needs=None):
                    link(COEF, coef_link, img, name, ins_of, needs)

                c("scaled", lambda: V.tensor_scalar(scaled[:], shared[0:C, 4:4 + PARTS], 2.0 / 3.0, -2.0,
                                                    ALU.mult, ALU.max))
                c("coef", lambda: V.tensor_scalar(coef[:], scaled[:], 2.0, rs[:, 0:1], ALU.min, ALU.mult))

                wait(dve, f2_ready, plus(img, -1), NB, 0)
                whole = [wmix[p][0:C, i].rearrange("k j r -> k (j r)") for i in range(2)]
                for i in range(2):
                    c(f"p{i}", lambda: V.scalar_tensor_tensor(
                        out=whole[i], in0=shift_sb[:], scalar=coef[:, 2 * i + 1:2 * i + 2], in1=eye_sb[:],
                        op0=ALU.mult, op1=ALU.add), "coef")
                for i in range(2):
                    c(f"i{i}", lambda: V.scalar_tensor_tensor(
                        out=whole[i], in0=eye_sb[:], scalar=coef[:, 2 * i:2 * i + 1], in1=whole[i],
                        op0=ALU.mult, op1=ALU.add), f"p{i}")

            def coef_row(img):
                p = img[1]

                def c(name, ins_of, needs=None):
                    link(COEF, coef_link, img, name, ins_of, needs)

                c("crow", lambda: V.tensor_copy(wmix[p][ONES:ONES + 1].rearrange("k i j r -> k (i j r)"),
                                                shared[ONES:ONES + 1, 64:64 + 2 * C]))

            def maximum(img, b):
                p = img[1]
                if not isinstance(img[0], int) or img[0] > 0:
                    dve.wait_ge(stored[p][b], img[0] * 16)
                wait(dve, f1_evacuated, img, NB, b + 1)
                wait(dve, f2_ready, img, NB, b + 1)
                V.scalar_tensor_tensor(out=x1[p][:, b], in0=f2[:, :, 0:BW], scalar=0.0, in1=f1_sb[:],
                                       op0=ALU.add, op1=ALU.max,
                                       accum_out=sums[p][:, 0, b:b + 1]).then_inc(x1_ready, 1)

            def norm_moments(img):
                p = img[1]

                def c(name, ins_of):
                    link(NORM, norm_link, img, name, ins_of)

                c("reduced", lambda: V.tensor_reduce(
                    me[p][:], shared[:, 256:256 + 2 * NB].rearrange("p (s b) -> p s b", s=2), AX.X, ALU.add))
                c("dev", lambda: V.tensor_scalar(dev[:], me[p][:, 0:1], negk[p][:, 0:1], None, ALU.add))
                c("ndev2", lambda: V.tensor_scalar(ndev2[:], dev[:], dev[:, 0:1], -1.0, ALU.mult, ALU.mult))
                c("veps", lambda: V.scalar_tensor_tensor(out=veps1[:], in0=me[p][:, 1:2], scalar=EPS, in1=ndev2[:],
                                                         op0=ALU.add, op1=ALU.add))

            def norm_bias(img):
                p = img[1]

                def c(name, ins_of):
                    link(NORM, norm_link, img, name, ins_of)

                c("nbias", lambda: V.tensor_scalar(nbias[p][:], me[p][:, 0:1], rs1[p][:, 0:1], -1.0,
                                                   ALU.mult, ALU.mult))

            def box_step(img, name, ins_of):
                link(BOX, box_link, img, name, ins_of)

            def box_t(img):
                box_step(img, "t", lambda: V.tensor_scalar(box["t"][:], shared[0:H, 128:128 + W], ALPHA, K_CONST,
                                                           ALU.mult, ALU.add))

            def box_t_root(img):
                box_step(img, "t_root", lambda: V.tensor_tensor(box["t_root"][:], box["t"][:], box["root"][:], ALU.mult))

            def box_power(img):
                box_step(img, "d0", lambda: V.reciprocal(box["d0"][:], box["root2"][:]))

            def box_halves(img):
                wait(dve, d_ready, img, NB, 0)
                box_step(img, "hi", lambda: V.tensor_copy(d_hi[:], box["d"][:]))
                box_step(img, "lo", lambda: V.tensor_tensor(d_lo[:], box["d"][:], d_hi[:], ALU.subtract))

            def scale(img, b):
                p = img[1]
                wait(dve, e_ready, img, NB, b + 1)
                V.scalar_tensor_tensor(out=x1[p][:, b], in0=x1[p][:, b], scalar=me[p][:, 0:1],
                                       in1=d_buffer(img, b)[:, None, 0:BW].to_broadcast([P, J, BW]),
                                       op0=ALU.subtract, op1=ALU.mult).then_inc(scaled_ready, 1)

            for i in range(EARLY):
                statistics((0, 0), i)
            def body(img):
                prev, nxt = plus(img, -1), plus(img, 1)
                begun = False
                for b, name, i in numbered(DVE_PLAN):
                    begun = begun or name == "coef_begin"
                    what, which, *args = {
                        "maximum": (maximum, *before(img, b)), "scale": (scale, *behind(img, b)),
                        "norm_moments": (norm_moments, prev), "norm_bias": (norm_bias, prev),
                        "statistics": (statistics, plus(img, 2), i - NB * Q + EARLY) if begun else
                                      (statistics, nxt, i + EARLY),
                        "coef_begin": (coef_begin, nxt), "coef_centre": (coef_centre, nxt),
                        "coef_veps": (coef_veps, nxt), "coef_y": (coef_y, nxt), "coef_hid": (coef_hid, nxt),
                        "coef_end": (coef_end, nxt), "coef_row": (coef_row, nxt),
                        "box_t": (box_t, prev), "box_t_root": (box_t_root, prev), "box_power": (box_power, prev),
                        "box_halves": (box_halves, prev)}[name]
                    if exists(which):
                        what(which, *args)
                if isinstance(img[0], int) and img == (FIRST // 2, FIRST % 2):
                    dve.wait_ge(consts_in, 16 * len(CONSTS))
                    V.tensor_copy(onehot_sb[:], onehot_f[:, :, :, None].to_broadcast([H, QROWS, Q, 32]),
                                  saturate=False).then_inc(onehot_set, 1)

            iterations(dve, body)

        @block.tensor
        def _(pe):
            T = nc.tensor

            def mix(img, b, i, j):
                p = img[1]
                if j == 0:
                    if b == 0 and i == 0:
                        after(pe, COEF, coef_link, img, "crow")
                        if isinstance(img[0], int) and img == (0, 1):
                            pe.wait_ge(ones_set, 2)
                    wait(pe, (f1_evacuated, x1_ready)[i], img, NB, b)
                dst = (f1, f2)[i]
                for q in range(Q):
                    last = T.matmul(dst[32 * q:32 * q + 32, j, 0:BW], wmix[p][:, i, j, :], xin[p][:, b, q, :],
                                    start=True, stop=True)
                if j == J - 1:
                    last.then_inc((f1_ready, f2_ready)[i], 1)

            def coef_groups(img):
                after(pe, BOX, box_link, plus(img, -2), "t")
                after(pe, COEF, coef_link, img, "aggr")
                T.matmul(shared[0:C, 8:9], dev96_sb[:], mv[:, 0:1], start=True, stop=True)
                T.matmul(shared[0:C, 0:1], g96_sb[:], mv[:, 0:1], start=True, stop=True)
                T.matmul(shared[:, 1:2], g96k_sb[:], mv[:, 0:1], start=True, stop=True).then_inc(coef_link, 1)

            def coef_var(img):
                after(pe, COEF, coef_link, img, "spread")
                T.matmul(shared[0:C, 2:3], g96_sb[:], spread[:], start=True, stop=True).then_inc(coef_link, 1)

            def coef_y(img):
                after(pe, COEF, coef_link, img, "y")
                T.matmul(shared[0:SQ, 3:4], w1t_sb[:], y[:], start=True, stop=True).then_inc(coef_link, 1)

            def coef_mlp(img):
                after(pe, COEF, coef_link, img, "hid")
                for s in range(PARTS):
                    last = T.matmul(shared[0:C, 4 + s:5 + s], w2t_sb[:, s, :], hid[:], start=True, stop=True)
                last.then_inc(coef_link, 1)

            def coef_row(img):
                after(pe, COEF, coef_link, img, "i1")
                for i in range(2):
                    row = shared[ONES:ONES + 1, 64 + i * C:64 + i * C + C]
                    T.matmul(row, nmean[:], wmix[img[1]][0:C, i].rearrange("k j r -> k (j r)"), start=True, stop=False)
                    last = T.matmul(row, nmean[:], neg_eye_sb[:], start=False, stop=True)
                last.then_inc(coef_link, 1)

            def group_sums(img):
                wait(pe, x1_ready, img, NB, NB)
                wait(pe, sumsq_ready, img, NB, NB)
                begins(pe, NORM, norm_link, img)
                T.matmul(shared[:, 256:256 + 2 * NB], g128_sb[:], sums[img[1]][:].rearrange("p s b -> p (s b)"),
                         start=True, stop=True).then_inc(norm_link, 1)

            def channel_sum(img, b):
                wait(pe, squares_ready if is_last(img) else group_squares_ready, img, NB, b + 1)
                if isinstance(img[0], int) and img == (0, 0) and b == 0:
                    pe.wait_ge(onehot_set, 1)
                channels = range(J if is_last(img) else 1)
                for t in range(ROWS):
                    for j in channels:
                        last = T.matmul(shared[32 * t:32 * t + 32, 0:W], quarter_sb[:, b, :],
                                        squares[b % 3][:, j, t * W:t * W + W], start=(b == 0 and j == 0),
                                        stop=(b == NB - 1 and j == channels[-1]))
                last.then_inc(chansum_ready, 1)

            def box_vert(img):
                after(pe, BOX, box_link, img, "sums")
                T.matmul(shared[0:W, 0:H], s_sb[:], vband_sb[:], start=True, stop=True).then_inc(box_link, 1)

            def box_full(img):
                after(pe, BOX, box_link, img, "vert")
                T.matmul(shared[0:H, 128:128 + W], box["vert"][:], band_sb[:], start=True, stop=True).then_inc(box_link, 1)

            def spread_d(img, b):
                if b == 0:
                    after(pe, BOX, box_link, img, "lo")
                wait_apart(pe, scaled_ready, img, NB, max(b - 1, 0) if is_last(img) else b, pe_passed)
                if is_last(img) and b == 1:
                    wait(pe, f1_evacuated, img, NB, NB)
                for t in range(ROWS):
                    rows = onehot_sb[:, ROWS * b + t].rearrange("h q r -> h (q r)")
                    for half in (d_hi, d_lo):
                        last = T.matmul(d_buffer(img, b)[:, t * W:t * W + W], rows, half[:], start=(half is d_hi),
                                        stop=(half is d_lo))
                last.then_inc(d_ready, 1)

            pe.wait_ge(consts_in, 16 * len(CONSTS))
            pe.wait_ge(ones_set, 1)

            def body(img):
                prev, nxt = plus(img, -1), plus(img, 1)
                for b, name, i in numbered(PE_PLAN):
                    what, which, *args = {
                        "mix": (mix, img, b, i // J % 2, i % J), "spread": (spread_d, *behind(img, b)),
                        "group_sums": (group_sums, prev), "channel_sum": (channel_sum, prev, i),
                        "box_vert": (box_vert, prev), "box_full": (box_full, prev),
                        "coef_groups": (coef_groups, nxt), "coef_var": (coef_var, nxt), "coef_y": (coef_y, nxt),
                        "coef_mlp": (coef_mlp, nxt), "coef_row": (coef_row, nxt)}[name]
                    if exists(which):
                        what(which, *args)

            iterations(pe, body)


def constants():
    cg = C // 6
    idx = np.arange(C).reshape(6, cg)
    idx = np.concatenate([idx[1:], idx[:1]], axis=0)
    idx = np.concatenate([idx[:, 1:], idx[:, :1]], axis=1).reshape(C)
    chan = np.array([J * r + j for j in range(J) for r in range(GROUPS)])
    f = np.float32
    k = np.arange(C)[:, None]
    eye = (k == chan[None, :]).astype(np.float16)
    neg_eye = -eye.astype(np.float32)
    shift = (k == idx[chan][None, :]).astype(np.float16)
    g96 = (k // J == k.T // J).astype(f) / f(J)
    dev96 = np.eye(C, dtype=f) - g96
    part = np.arange(P)
    g96k = (k // J == part[None, :] % GROUPS).astype(f) / f(J)
    g128 = (part[:, None] % GROUPS == part[None, :] % GROUPS).astype(f) / f(J * HW)
    col = np.arange(32)
    quarter = ((col[None, None, :] // Q == np.arange(NB)[None, :, None])
               & (col[None, None, :] % Q == part[:, None, None] // GROUPS)).astype(f)
    t, b, q = part // 32, part % 32 // Q, part % Q
    row = np.where(b < NB, QROWS * q + ROWS * b + t, -1000)
    vband = (np.abs(row[:, None] - np.arange(H)[None, :]) <= 2).astype(f)
    band = (np.abs(np.arange(W)[:, None] - np.arange(W)[None, :]) <= 2).astype(f)
    onehot = (np.arange(H)[:, None, None] == QROWS * np.arange(Q)[None, None, :] + np.arange(QROWS)[None, :, None]).astype(f)
    return dict(eye=eye, neg_eye=neg_eye, shift=shift, g96=g96, dev96=dev96, g96k=g96k, g128=g128, quarter=quarter, vband=vband, band=band,
                onehot=onehot), np.argsort(idx)


def kernel(x, L0_conv_W1, L0_conv_b1, L0_conv_W2, L0_conv_b2):
    import concourse.bacc as bacc
    from concourse.bass_utils import run_bass_kernel_spmd

    tables, reader = constants()
    order = [np.arange(C), reader, np.arange(C), reader]
    w2 = np.asarray(L0_conv_W2).reshape(PARTS, C, SQ)
    b2 = np.asarray(L0_conv_b2).reshape(PARTS, C)
    arrays = {
        "x": np.asarray(x),
        "w1t": np.ascontiguousarray(np.asarray(L0_conv_W1).T),
        "b1": np.asarray(L0_conv_b1).reshape(SQ, 1),
        "w2t": np.concatenate([np.stack([w2[s][order[s]] for s in range(PARTS)]).transpose(2, 0, 1),
                               np.stack([b2[s][order[s]] for s in range(PARTS)])[None]], axis=0),
        **tables,
    }
    nc = bacc.Bacc("TRN2", target_bir_lowering=False, num_devices=1)
    args = [nc.dram_tensor(f"in_{n}", a.shape, mybir.dt.from_np(a.dtype), kind="ExternalInput").ap()
            for n, a in arrays.items()]
    args.append(nc.dram_tensor("out", (B, C, H, W), mybir.dt.float32, kind="ExternalOutput").ap())
    build(nc, *args)
    r = run_bass_kernel_spmd(nc, [{f"in_{n}": a for n, a in arrays.items()}], core_ids=[0])
    return r.results[0]["out"]
```
